# Optimizing a Trainium2 kernel written in Bass

```python
import numpy as np
import jax
import jax.numpy as jnp

def _softmax(x, axis=-1):
    return jax.nn.softmax(x, axis=axis)

def _gelu(x):
    return jax.nn.gelu(x, approximate=True)

def _silu(x):
    return jax.nn.silu(x)

def _sigmoid(x):
    return jax.nn.sigmoid(x)

def _layernorm(x, axis=-1, eps=1e-05):
    m = jnp.mean(x, axis=axis, keepdims=True)
    v = jnp.var(x, axis=axis, keepdims=True)
    return (x - m) / jnp.sqrt(v + eps)

def _scatter_add(tgt, idx, src, axis=0):
    return tgt.at[idx].add(src)

def _segment_sum(src, seg, n):
    return jax.ops.segment_sum(src, seg, n)
kernel_name = 'mk_cond_seq_d2_seqx_r8_aa92ee'

def setup_inputs(seed: int=0):
    np.random.seed(seed)
    _w = jnp.asarray

    def _rec_inputs():
        import jax
        import jax.numpy as jnp
        _rk = jax.random.key(seed)
        x = -0.000125 + 0.9999 * jax.random.normal(jax.random.fold_in(_rk, 1), (4, 256, 128), jnp.float32)
        _lenS = 256 - jax.random.randint(jax.random.fold_in(_rk, 7), (4,), 0, max(1, 256 // 4) + 1, jnp.int32)
        _lenS2 = 256 - jax.random.randint(jax.random.fold_in(_rk, 8), (4,), 0, max(1, 256 // 4) + 1, jnp.int32)
        itok_B_0_15 = jax.random.randint(jax.random.fold_in(_rk, 11), (4,), 0, 16, jnp.int32)
        itok_B_6_14 = jax.random.randint(jax.random.fold_in(_rk, 12), (4,), 6, 15, jnp.int32)
        return (x, itok_B_0_15, itok_B_6_14)
    x, itok_B_0_15, itok_B_6_14 = _rec_inputs()

    def _L0_cond_setup():
        import jax, jax.numpy as jnp
        import numpy as np
        B, S, D = (32, 128, 128)
        A = 32
        E = 16
        LN_EPS = 1e-05
        key = jax.random.key(seed)
        ks = jax.random.split(key, 10)
        s = lambda fan_in: 1.0 / np.sqrt(fan_in)
        return {'hidden_states': jax.random.normal(ks[0], (B, S, D), dtype=jnp.float32), 'domain_id': jax.random.randint(ks[1], (B,), 0, E, dtype=jnp.int64), 'down_W': jax.random.uniform(ks[2], (A, D), jnp.float32, -s(D), s(D)), 'down_b': jax.random.uniform(ks[3], (A,), jnp.float32, -s(D), s(D)), 'up_W': jax.random.uniform(ks[4], (D, A), jnp.float32, -s(A), s(A)), 'up_b': jax.random.uniform(ks[5], (D,), jnp.float32, -s(A), s(A)), 'expert_W': jax.random.uniform(ks[6], (E, A, A), jnp.float32, -s(A), s(A)), 'expert_b': jax.random.uniform(ks[7], (E, A), jnp.float32, -s(A), s(A)), 'domain_emb': jax.random.normal(ks[8], (E, A), dtype=jnp.float32), 'ln_gamma': jnp.ones((D,), jnp.float32), 'ln_beta': jnp.zeros((D,), jnp.float32)}
    _L0_cond_all = _L0_cond_setup()
    _L0_cond_in = {k: v for k, v in _L0_cond_all.items() if k in ('down_W', 'down_b', 'up_W', 'up_b', 'expert_W', 'expert_b', 'domain_emb', 'ln_gamma', 'ln_beta')}
    del _L0_cond_all

    def _L1_cond_setup():
        import jax, jax.numpy as jnp
        import numpy as np
        D = 128
        E = 8
        FF = 512
        TOPK = 2
        S = 32
        SE = 64
        SH = 128
        B, T = (2, 256)

        def _forward(x, subject_ids, ln_g, ln_b, subj_emb, hyp_w1, hyp_b1, hyp_w2, hyp_b2, sty_w1, sty_b1, sty_w2, sty_b2, router_w, exp_w1, exp_b1, exp_w2, exp_b2):
            mu = x.mean(-1, keepdims=True)
            var = x.var(-1, keepdims=True)
            h = (x - mu) * jax.lax.rsqrt(var + 1e-05) * ln_g + ln_b
            m_t = h.mean(1, keepdims=True)
            v_t = h.var(1, keepdims=True)
            h_norm = (h - m_t) * jax.lax.rsqrt(v_t + 1e-08)
            se = subj_emb[subject_ids]
            hyp = jax.nn.relu(se @ hyp_w1 + hyp_b1) @ hyp_w2 + hyp_b2
            sty = jax.nn.relu(hyp @ sty_w1 + sty_b1) @ sty_w2 + sty_b2
            gamma, beta = jnp.split(sty, 2, axis=-1)
            gamma = jax.nn.softplus(gamma) + 1e-08
            h = h_norm * gamma[:, None, :] + beta[:, None, :]
            h_flat = h.reshape(-1, D)
            probs = jax.nn.softmax(h_flat @ router_w, axis=-1)
            gates, idx = jax.lax.top_k(probs, TOPK)
            gates = gates / gates.sum(-1, keepdims=True)
            N = h_flat.shape[0]
            combine = jnp.zeros((N, E), h_flat.dtype).at[jnp.arange(N)[:, None], idx].add(gates)
            hid = jax.nn.relu(jnp.einsum('nd,edf->nef', h_flat, exp_w1) + exp_b1)
            eout = jnp.einsum('nef,efd->ned', hid, exp_w2) + exp_b2
            y = jnp.einsum('ned,ne->nd', eout, combine)
            return x + y.reshape(x.shape)
        key = jax.random.key(seed)
        ks = jax.random.split(key, 16)
        n = lambda k, sh, s=0.02: jax.random.normal(k, sh, dtype=jnp.float32) * s
        return {'x': jax.random.normal(ks[0], (B, T, D), dtype=jnp.float32), 'subject_ids': jax.random.randint(ks[1], (B,), 0, S), 'ln_g': jnp.ones((D,), jnp.float32), 'ln_b': jnp.zeros((D,), jnp.float32), 'subj_emb': n(ks[2], (S, SE)), 'hyp_w1': n(ks[3], (SE, SH), 1.0 / np.sqrt(SE)), 'hyp_b1': jnp.zeros((SH,), jnp.float32), 'hyp_w2': n(ks[4], (SH, SH), 1.0 / np.sqrt(SH)), 'hyp_b2': jnp.zeros((SH,), jnp.float32), 'sty_w1': n(ks[5], (SH, SH // 2), 1.0 / np.sqrt(SH)), 'sty_b1': jnp.zeros((SH // 2,), jnp.float32), 'sty_w2': n(ks[6], (SH // 2, 2 * D), 1.0 / np.sqrt(SH // 2)), 'sty_b2': jnp.zeros((2 * D,), jnp.float32), 'router_w': n(ks[7], (D, E), 1.0 / np.sqrt(D)), 'exp_w1': n(ks[8], (E, D, FF), 1.0 / np.sqrt(D)), 'exp_b1': jnp.zeros((E, FF), jnp.float32), 'exp_w2': n(ks[9], (E, FF, D), 1.0 / np.sqrt(FF)), 'exp_b2': jnp.zeros((E, D), jnp.float32)}
    _L1_cond_all = _L1_cond_setup()
    _L1_cond_in = {k: v for k, v in _L1_cond_all.items() if k in ('ln_g', 'ln_b', 'subj_emb', 'hyp_w1', 'hyp_b1', 'hyp_w2', 'hyp_b2', 'sty_w1', 'sty_b1', 'sty_w2', 'sty_b2', 'router_w', 'exp_w1', 'exp_b1', 'exp_w2', 'exp_b2')}
    del _L1_cond_all
    return {'x': x, 'itok_B_0_15': itok_B_0_15, 'itok_B_6_14': itok_B_6_14, 'L0_cond_down_W': _L0_cond_in['down_W'], 'L0_cond_down_b': _L0_cond_in['down_b'], 'L0_cond_up_W': _L0_cond_in['up_W'], 'L0_cond_up_b': _L0_cond_in['up_b'], 'L0_cond_expert_W': _L0_cond_in['expert_W'], 'L0_cond_expert_b': _L0_cond_in['expert_b'], 'L0_cond_domain_emb': _L0_cond_in['domain_emb'], 'L0_cond_ln_gamma': _L0_cond_in['ln_gamma'], 'L0_cond_ln_beta': _L0_cond_in['ln_beta'], 'L1_cond_ln_g': _L1_cond_in['ln_g'], 'L1_cond_ln_b': _L1_cond_in['ln_b'], 'L1_cond_subj_emb': _L1_cond_in['subj_emb'], 'L1_cond_hyp_w1': _L1_cond_in['hyp_w1'], 'L1_cond_hyp_b1': _L1_cond_in['hyp_b1'], 'L1_cond_hyp_w2': _L1_cond_in['hyp_w2'], 'L1_cond_hyp_b2': _L1_cond_in['hyp_b2'], 'L1_cond_sty_w1': _L1_cond_in['sty_w1'], 'L1_cond_sty_b1': _L1_cond_in['sty_b1'], 'L1_cond_sty_w2': _L1_cond_in['sty_w2'], 'L1_cond_sty_b2': _L1_cond_in['sty_b2'], 'L1_cond_router_w': _L1_cond_in['router_w'], 'L1_cond_exp_w1': _L1_cond_in['exp_w1'], 'L1_cond_exp_b1': _L1_cond_in['exp_b1'], 'L1_cond_exp_w2': _L1_cond_in['exp_w2'], 'L1_cond_exp_b2': _L1_cond_in['exp_b2']}

def reference(x, itok_B_0_15, itok_B_6_14, L0_cond_down_W, L0_cond_down_b, L0_cond_up_W, L0_cond_up_b, L0_cond_expert_W, L0_cond_expert_b, L0_cond_domain_emb, L0_cond_ln_gamma, L0_cond_ln_beta, L1_cond_ln_g, L1_cond_ln_b, L1_cond_subj_emb, L1_cond_hyp_w1, L1_cond_hyp_b1, L1_cond_hyp_w2, L1_cond_hyp_b2, L1_cond_sty_w1, L1_cond_sty_b1, L1_cond_sty_w2, L1_cond_sty_b2, L1_cond_router_w, L1_cond_exp_w1, L1_cond_exp_b1, L1_cond_exp_w2, L1_cond_exp_b2):
    import jax
    import jax.numpy as jnp

    def _L0_cond_ref(hidden_states, domain_id, down_W, down_b, up_W, up_b, expert_W, expert_b, domain_emb, ln_gamma, ln_beta):
        import jax, jax.numpy as jnp
        import numpy as np
        B, S, D = (32, 128, 128)
        A = 32
        E = 16
        LN_EPS = 1e-05
        residual = hidden_states
        hidden = jnp.einsum('bsd,ad->bsa', hidden_states, down_W) + down_b
        hidden = jax.nn.gelu(hidden, approximate=False)
        valid = (domain_id >= 0) & (domain_id < E)
        idx = jnp.clip(domain_id, 0, E - 1)
        Wsel = expert_W[idx]
        bsel = expert_b[idx]
        expert_out = jnp.einsum('bsa,boa->bso', hidden, Wsel) + bsel[:, None, :]
        domain_output = jnp.where(valid[:, None, None], expert_out, hidden)
        hidden = domain_output + domain_emb[idx][:, None, :]
        hidden = jnp.einsum('bsa,da->bsd', hidden, up_W) + up_b
        x = hidden + residual
        mu = jnp.mean(x, axis=-1, keepdims=True)
        var = jnp.mean(jnp.square(x - mu), axis=-1, keepdims=True)
        return (x - mu) * jax.lax.rsqrt(var + LN_EPS) * ln_gamma + ln_beta

    def _L1_cond_ref(x, subject_ids, ln_g, ln_b, subj_emb, hyp_w1, hyp_b1, hyp_w2, hyp_b2, sty_w1, sty_b1, sty_w2, sty_b2, router_w, exp_w1, exp_b1, exp_w2, exp_b2):
        import jax, jax.numpy as jnp
        import numpy as np
        D = 128
        E = 8
        FF = 512
        TOPK = 2
        S = 32
        SE = 64
        SH = 128
        B, T = (2, 256)

        def _forward(x, subject_ids, ln_g, ln_b, subj_emb, hyp_w1, hyp_b1, hyp_w2, hyp_b2, sty_w1, sty_b1, sty_w2, sty_b2, router_w, exp_w1, exp_b1, exp_w2, exp_b2):
            mu = x.mean(-1, keepdims=True)
            var = x.var(-1, keepdims=True)
            h = (x - mu) * jax.lax.rsqrt(var + 1e-05) * ln_g + ln_b
            m_t = h.mean(1, keepdims=True)
            v_t = h.var(1, keepdims=True)
            h_norm = (h - m_t) * jax.lax.rsqrt(v_t + 1e-08)
            se = subj_emb[subject_ids]
            hyp = jax.nn.relu(se @ hyp_w1 + hyp_b1) @ hyp_w2 + hyp_b2
            sty = jax.nn.relu(hyp @ sty_w1 + sty_b1) @ sty_w2 + sty_b2
            gamma, beta = jnp.split(sty, 2, axis=-1)
            gamma = jax.nn.softplus(gamma) + 1e-08
            h = h_norm * gamma[:, None, :] + beta[:, None, :]
            h_flat = h.reshape(-1, D)
            probs = jax.nn.softmax(h_flat @ router_w, axis=-1)
            gates, idx = jax.lax.top_k(probs, TOPK)
            gates = gates / gates.sum(-1, keepdims=True)
            N = h_flat.shape[0]
            combine = jnp.zeros((N, E), h_flat.dtype).at[jnp.arange(N)[:, None], idx].add(gates)
            hid = jax.nn.relu(jnp.einsum('nd,edf->nef', h_flat, exp_w1) + exp_b1)
            eout = jnp.einsum('nef,efd->ned', hid, exp_w2) + exp_b2
            y = jnp.einsum('ned,ne->nd', eout, combine)
            return x + y.reshape(x.shape)
        return _forward(x, subject_ids, ln_g, ln_b, subj_emb, hyp_w1, hyp_b1, hyp_w2, hyp_b2, sty_w1, sty_b1, sty_w2, sty_b2, router_w, exp_w1, exp_b1, exp_w2, exp_b2)
    x = _L0_cond_ref(x, itok_B_0_15, L0_cond_down_W, L0_cond_down_b, L0_cond_up_W, L0_cond_up_b, L0_cond_expert_W, L0_cond_expert_b, L0_cond_domain_emb, L0_cond_ln_gamma, L0_cond_ln_beta)
    x = _L1_cond_ref(x, itok_B_6_14, L1_cond_ln_g, L1_cond_ln_b, L1_cond_subj_emb, L1_cond_hyp_w1, L1_cond_hyp_b1, L1_cond_hyp_w2, L1_cond_hyp_b2, L1_cond_sty_w1, L1_cond_sty_b1, L1_cond_sty_w2, L1_cond_sty_b2, L1_cond_router_w, L1_cond_exp_w1, L1_cond_exp_b1, L1_cond_exp_w2, L1_cond_exp_b2)
    return x

_drawn_inputs = setup_inputs


def setup_inputs(seed=0):
    import zlib

    import numpy as np

    out = dict(_drawn_inputs(seed))
    spreads = {'L0_cond_ln_gamma': (1.0, 0.2),
     'L0_cond_ln_beta': (0.0, 0.1),
     'L1_cond_ln_g': (1.0, 0.2),
     'L1_cond_ln_b': (0.0, 0.1),
     'L1_cond_hyp_b1': (0.0, 0.1),
     'L1_cond_hyp_b2': (0.0, 0.1),
     'L1_cond_sty_b1': (0.0, 0.1),
     'L1_cond_sty_b2': (0.0, 0.1),
     'L1_cond_exp_b1': (0.0, 0.1),
     'L1_cond_exp_b2': (0.0, 0.1)}
    factors = {}
    for name, (base, spread) in spreads.items():
        noise = np.random.default_rng([zlib.crc32(name.encode()), seed]).standard_normal(out[name].shape)
        drawn = base * np.exp(spread * noise) if base else spread * noise
        out[name] = jnp.asarray(drawn.astype(out[name].dtype))
    for name, factor in factors.items():
        out[name] = (out[name] * factor).astype(out[name].dtype)
    return out
```

```python
from contextlib import ExitStack

import numpy as np

import concourse.bass as bass
from concourse import mybir

F32 = mybir.dt.float32
F32R = mybir.dt.float32r
I32 = mybir.dt.int32
ALU = mybir.AluOpType
ACT = mybir.ActivationFunctionType
AX = mybir.AxisListType.X

P = 128
B, S, D = 4, 256, 128
N = B * S
T = S // P
J = B * T
HALVES = 2
HN = N // HALVES
HB = B // HALVES
HJ = J // HALVES
A, DOMAINS = 32, 16
E, FF = 8, 512
FC = FF // P
SUBJ, SE, SH, SC = 32, 64, 128, 64
UNITS = HALVES * FC
RING = 4
LEAD = 2
LN_EPS, IN_EPS = 1e-5, 1e-8

C_B1, C_B2 = 0, E * UNITS
C_LNG, C_LNB, C_HB1, C_HB2, C_SB1, C_SBG, C_SBB, C_DB = range(C_B2 + E, C_B2 + E + 8)
COLS = C_DB + 1


class Packed:

    def __init__(self, **widths):
        self.at, self.width = {}, 0
        for name, width in widths.items():
            self.at[name] = (self.width, self.width + width)
            self.width += width

    def of(self, tile, name, rows=P):
        a, b = self.at[name]
        return tile[0:rows, a:b]


EARLY = Packed(down=A, cols=COLS)
DOMAIN = Packed(up=D, expert=A * DOMAINS, expert_b=A, emb=A, up_b=D)
STYLE = Packed(subj=SE, hyp1=SH, hyp2=SH, sty1=SC, sty2=2 * D, router=E)


class Count:

    def __init__(self):
        self.n = 0

    def add(self, k=1):
        self.n += k
        return k


def adapter_moe(nc, x, ids, early, domain, style, ln_row, w_all, out):
    ctx = ExitStack()
    with ctx:
        def sb(name, shape, dt=F32):
            return ctx.enter_context(nc.sbuf_tensor(name, shape, dt))

        def sem(name):
            return ctx.enter_context(nc.semaphore(name))

        x_sb = sb("x_sb", [P, J, D])
        xT = sb("xT", [P, HALVES, HN])
        early_sb = sb("early_sb", [P, EARLY.width])
        domain_sb = sb("domain_sb", [P, DOMAIN.width])
        style_sb = sb("style_sb", [P, STYLE.width])
        ln0_sb = sb("ln0_sb", [P, 2, D])
        ids_i = sb("ids_i", [SUBJ, 2 * B], I32)
        ident = sb("ident", [P, P])
        lane = sb("lane", [P, 1])
        rank = sb("rank", [P, E])
        in_sample = sb("in_sample", [P, B])
        in_pair = sb("in_pair", [P, HB])
        row_of = sb("row_of", [B, B, P])
        ones = sb("ones", [1, B])
        eye_a = sb("eye_a", [P, A])
        ids_f = sb("ids_f", [SUBJ, 2 * B])
        id_t = sb("id_t", [SUBJ, 4, 2 * B])
        onehot_d = sb("onehot_d", [DOMAINS, B])
        onehot_v = sb("onehot_v", [DOMAINS, B])
        onehot_x = sb("onehot_x", [DOMAINS, B, A])
        onehot_s = sb("onehot_s", [SUBJ, B])
        pick = sb("pick", [P, DOMAINS])
        picked = sb("picked", [P, A, DOMAINS])
        w_sel = sb("w_sel", [P, A])
        invalid = sb("invalid", [P, 2])
        w_eff = sb("w_eff", [P, A])
        w_diag = sb("w_diag", [P, B, A])
        bias_T = sb("bias_T", [A, B])
        bias_row = sb("bias_row", [B, D])
        up_diag = sb("up_diag", [P, HB, D])
        hidden_T = sb("hidden_T", [P, S])
        se_T = sb("se_T", [SE, B])
        hyp1_T = sb("hyp1_T", [SH, B])
        hyp2_T = sb("hyp2_T", [SH, B])
        sty1_T = sb("sty1_T", [SC, B])
        gamma_raw = sb("gamma_raw", [P, B])
        beta_T = sb("beta_T", [P, B])
        soft = sb("soft", [P, 3, B])
        gamma_T = sb("gamma_T", [P, B])
        res = sb("res", [P, J, D])
        x1 = sb("x1", [P, J, D])
        stats = sb("stats", [P, J, 6])
        mv = sb("mv", [P, J, 2])
        std = sb("std", [P, J])
        rstd = sb("rstd", [P, J])
        z = sb("z", [P, J, D])
        g2 = sb("g2", [P, 1])
        t_stats = sb("t_stats", [P, B, 6])
        t_mv = sb("t_mv", [P, B, 2])
        t_small = sb("t_small", [P, 8, B])
        scale_T = sb("scale_T", [P, B])
        shift_T = sb("shift_T", [P, B])
        h_full = sb("h_full", [P, B, S])
        h_high = sb("h_high", [P, B, S], F32R)
        h_low = sb("h_low", [P, B, S], F32R)
        gt = sb("gt", [P, 8, J, E])
        gs = sb("gs", [P, 10, J])
        gates = sb("gates", [P, J, E])
        gates_T = sb("gates_T", [E, N])
        gate_all = sb("gate_all", [P, E, N])
        w_raw = sb("w_raw", [P, E, 2 * FF])
        w_high = sb("w_high", [P, 2 * FF], F32R)
        w_low = sb("w_low", [P, 2 * FF], F32R)
        hid_full = sb("hid_full", [P, RING, HN])
        hid_high = sb("hid_high", [P, RING, HN], F32R)
        hid_low = sb("hid_low", [P, RING, HN], F32R)
        y_part = sb("y_part", [P, HALVES, HN])
        y_sum = sb("y_sum", [P, HALVES, HN])
        out_sb = sb("out_sb", [P, J, D])
        scratch = nc.dram_tensor("gate_scratch", [E, N], F32, kind="Internal").ap()

        bank = [ctx.enter_context(nc.psum_tensor(f"bank{i}", [P, 512], F32)) for i in range(8)]
        hid_ps = bank[0:RING]
        y_ps = bank[RING:RING + HALVES]
        misc0, misc1 = bank[6], bank[7]
        xT_ps, up_ps, zT_ps = bank[0:2], bank[2:4], y_ps
        pick_ps = y_ps[0][:, 0:DOMAINS]
        bias_T_ps = misc0[0:A, 16:16 + B]
        bias_row_ps = misc0[0:B, 32:32 + D]
        up_eff_ps = y_ps[1][:, 0:D]
        down_ps = misc1[:, 0:S]
        se_ps, hyp1_ps, hyp2_ps, sty1_ps, gam_ps, bet_ps = (
            misc0[0:r, c:c + B] for r, c in ((SE, 256), (SH, 264), (SH, 272), (SC, 280), (P, 288), (P, 296)))
        logit_ps = misc1[:, 320:320 + J * E].rearrange("p (j e) -> p j e", e=E)

        cols = EARLY.of(early_sb, "cols")

        def col(c, rows=P):
            return cols[0:rows, c:c + 1]

        x_loaded = [sem(f"x_loaded{h}") for h in range(HALVES)]
        early_loaded, domain_loaded, style_loaded = sem("early_loaded"), sem("domain_loaded"), sem("style_loaded")
        ids_loaded, ln0_loaded = sem("ids_loaded"), sem("ln0_loaded")
        w0_loaded, w_loaded = sem("w0_loaded"), sem("w_loaded")
        pool_steps = sem("pool_steps")
        ident_ready, masks_ready = sem("ident_ready"), sem("masks_ready")
        vec_steps = sem("vec_steps")
        act_steps = sem("act_steps")
        xT_in_psum, xT_ready = sem("xT_in_psum"), sem("xT_ready")
        onehots_ready = sem("onehots_ready")
        pick_in_psum, bias_T_in_psum, bias_T_ready = sem("pick_in_psum"), sem("bias_T_in_psum"), sem("bias_T_ready")
        bias_row_in_psum, bias_row_ready = sem("bias_row_in_psum"), sem("bias_row_ready")
        w_diag_ready, up_eff_in_psum, up_diag_ready = sem("w_diag_ready"), sem("up_eff_in_psum"), sem("up_diag_ready")
        down_in_psum, gelu_ready, up_in_psum = sem("down_in_psum"), sem("gelu_ready"), sem("up_in_psum")
        style_in_psum, style_ready = sem("style_in_psum"), sem("style_ready")
        soft_in, soft_exp, soft_ln = sem("soft_in"), sem("soft_exp"), sem("soft_ln")
        up_taken = sem("up_taken")
        var_ready, std_ready = sem("var_ready"), sem("std_ready")
        z_ready, zT_in_psum = sem("z_ready"), sem("zT_in_psum")
        affine_ready, h_scaled, h_ready = sem("affine_ready"), sem("h_scaled"), sem("h_ready")
        logits_in_psum, logits_shifted, exps_ready = sem("logits_in_psum"), sem("logits_shifted"), sem("exps_ready")
        gates_ready, gates_T_in_psum, gates_T_ready = sem("gates_ready"), sem("gates_T_in_psum"), sem("gates_T_ready")
        gates_stored, gate0_loaded, gate_loaded = sem("gates_stored"), sem("gate0_loaded"), sem("gate_loaded")
        w_high_ready, w_low_ready = sem("w_high_ready"), sem("w_low_ready")
        hid_in_psum = sem("hid_in_psum")
        hid_rounded = sem("hid_rounded")
        hid_split = sem("hid_split")
        down_done = sem("down_done")
        y_taken, y_added = sem("y_taken"), sem("y_added")
        yT_in_psum, out_ready, out_stored = sem("yT_in_psum"), sem("out_ready"), sem("out_stored")

        x_dram = x.rearrange("b (t p) d -> p (b t) d", p=P)
        out_dram = out.rearrange("b (t p) d -> p (b t) d", p=P)

        block = ctx.enter_context(nc.Block())

        def quarter(q):
            return slice(q * 256, (q + 1) * 256)

        @block.sync
        def _(sp):
            for h in range(HALVES):
                sp.dma_start(x_sb[:, h * HJ:(h + 1) * HJ, :], x_dram[:, h * HJ:(h + 1) * HJ, :]).then_inc(x_loaded[h], 16)
            sp.dma_start(w_raw[:, 0, :], w_all[:, 0, :]).then_inc(w0_loaded, 16)
            sp.dma_start(w_raw[:, 1:E, :], w_all[:, 1:E, :]).then_inc(w_loaded, 16)
            sp.wait_ge(gates_T_ready, 2)
            sp.dma_start(scratch, gates_T[:, :]).then_inc(gates_stored, 16)
            sp.wait_ge(gates_stored, 16)
            sp.dma_start(gate_all[:, 0, :], scratch[0, :].partition_broadcast(P)).then_inc(gate0_loaded, 16)
            sp.dma_start(gate_all[:, 1:E, :],
                         scratch[1:E, :].rearrange("e n -> (e n)").partition_broadcast(P)).then_inc(gate_loaded, 16)
            for h in range(HALVES):
                sp.wait_ge(out_ready, h + 1)
                sp.dma_start(out_dram[:, h * HJ:(h + 1) * HJ, :], out_sb[:, h * HJ:(h + 1) * HJ, :]).then_inc(out_stored, 16)
            sp.wait_ge(out_stored, 16 * HALVES)

        @block.gpsimd
        def _(pool):
            steps = Count()

            def split_low(e, q, waited):
                pool.wait_ge(w0_loaded if isinstance(e, int) and e == 0 else w_loaded, 16)
                pool.wait_ge(w_high_ready, waited)
                nc.gpsimd.tensor_tensor(w_low[:, quarter(q)], w_raw[:, e, quarter(q)],
                                        w_high[:, quarter(q)].bitcast(F32), ALU.subtract).then_inc(w_low_ready, 1)

            def add_expert(e, h):
                pool.wait_ge(y_taken, HALVES * e + h + 1)
                nc.gpsimd.tensor_tensor(y_sum[:, h, :], y_sum[:, h, :], y_part[:, h, :], ALU.add).then_inc(y_added, 1)

            nc.gpsimd.memset(ident[:, :], 0.0).then_inc(pool_steps, steps.add())
            pool.wait_ge(pool_steps, steps.n)
            nc.gpsimd.affine_select(out=ident[:, :], in_=ident[:, :], compare_op=ALU.not_equal, fill=1.0,
                                    base=0, pattern=[[-1, P]], channel_multiplier=1).then_inc(ident_ready, 1)
            nc.gpsimd.iota(lane[:, :], pattern=[[0, 1]], base=0, channel_multiplier=1,
                           allow_small_or_imprecise_dtypes=True).then_inc(masks_ready, 1)
            nc.gpsimd.iota(rank[:, :], pattern=[[-1, E]], base=E, channel_multiplier=0,
                           allow_small_or_imprecise_dtypes=True).then_inc(masks_ready, 1)
            nc.gpsimd.memset(ones[:, :], 1.0).then_inc(masks_ready, 1)
            nc.gpsimd.memset(row_of[:, :, :], 1.0).then_inc(pool_steps, steps.add())
            nc.gpsimd.memset(in_sample[:, :], 1.0).then_inc(pool_steps, steps.add())
            pool.wait_ge(pool_steps, steps.n)
            nc.gpsimd.affine_select(out=row_of[:, :, :], in_=row_of[:, :, :], compare_op=ALU.is_equal, fill=0.0,
                                    base=0, pattern=[[-1, B], [0, P]], channel_multiplier=1).then_inc(masks_ready, 1)
            nc.gpsimd.affine_select(out=in_sample[:, :], in_=in_sample[:, :], compare_op=ALU.is_ge, fill=0.0,
                                    base=0, pattern=[[-A, B]], channel_multiplier=1).then_inc(pool_steps, steps.add())
            pool.wait_ge(pool_steps, steps.n)
            nc.gpsimd.affine_select(out=in_sample[:, :], in_=in_sample[:, :], compare_op=ALU.is_ge, fill=0.0,
                                    base=A - 1, pattern=[[A, B]], channel_multiplier=-1).then_inc(masks_ready, 1)

            for q in range(4):
                split_low(0, q, q + 1)
            for q in range(3):
                split_low(1, q, 4 + q + 1)
            pool.wait_ge(gate0_loaded, 16)
            for h in range(HALVES):
                pool.wait_ge(y_taken, h + 1)
                nc.gpsimd.tensor_tensor(y_sum[:, h, :], y_part[:, h, :], gate_all[:, 0, h * HN:(h + 1) * HN],
                                        ALU.mult).then_inc(y_added, 1)

            def expert(e, last=False):
                if not (isinstance(e, int) and e == 1):
                    add_expert(e - 1, 1)
                split_low(e, 3, 4 * e + 4)
                add_expert(e, 0)
                if not last:
                    for q in range(3):
                        split_low(e + 1, q, 4 * e + 4 + q + 1)

            expert(1)
            with pool.Fori(2, E - 1) as e:
                expert(e)
            expert(E - 1, last=True)
            add_expert(E - 1, 1)

        def relu_unit(act, e, u):
            unit = UNITS * e + u
            slot = u % RING
            act.wait_ge(early_loaded, 16)
            act.wait_ge(hid_in_psum, unit + 1)
            bias = cols[:, bass.ds(C_B1 + e * UNITS + u, 1)]
            nc.scalar.activation(hid_full[:, slot, :], hid_ps[slot][:, :], ACT.Relu, bias=bias).then_inc(hid_rounded, 1)
            nc.scalar.activation(hid_high[:, slot, :], hid_ps[slot][:, :], ACT.Relu, bias=bias).then_inc(hid_rounded, 1)

        @block.scalar
        def _(act):
            act.dma_start(ids_i[:, :], ids[0, :].partition_broadcast(SUBJ)).then_inc(ids_loaded, 16)
            act.dma_start(early_sb[:, :], early).then_inc(early_loaded, 16)
            act.dma_start(domain_sb[:, :], domain).then_inc(domain_loaded, 16)
            act.dma_start(style_sb[:, :], style).then_inc(style_loaded, 16)
            act.dma_start(ln0_sb[:, :, :], ln_row.rearrange("a b d -> a (b d)")[0, :].partition_broadcast(P)
                          ).then_inc(ln0_loaded, 16)
            nc.scalar.preload_act_table(ACT.Gelu)
            for h in range(HALVES):
                act.wait_ge(xT_in_psum, h + 1)
                nc.scalar.activation(xT[:, h, :], xT_ps[h][:, :], ACT.Copy).then_inc(xT_ready, 1)
            act.wait_ge(early_loaded, 16)
            for h in range(HALVES):
                rows = slice(h * HB * A, (h + 1) * HB * A)
                act.wait_ge(down_in_psum, h + 1)
                nc.scalar.activation(hidden_T[rows, :], down_ps[rows, :], ACT.Gelu,
                                     bias=cols[rows, C_DB:C_DB + 1]).then_inc(gelu_ready, 1)
            act.wait_ge(soft_in, 1)
            nc.scalar.activation(soft[:, 1, :], soft[:, 0, :], ACT.Exp).then_inc(soft_exp, 1)
            act.wait_ge(soft_exp, 1)
            nc.scalar.activation(soft[:, 2, :], soft[:, 1, :], ACT.Ln, bias=1.0).then_inc(soft_ln, 1)
            nc.scalar.preload_act_table(ACT.Sqrt)
            roots = Count()

            def root(dst, src):
                roots.add()
                act.wait_ge(var_ready, roots.n)
                nc.scalar.activation(dst, src, ACT.Sqrt).then_inc(std_ready, 1)

            for h in range(HALVES):
                tiles = slice(h * HJ, (h + 1) * HJ)
                root(std[:, tiles], std[:, tiles])
                root(std[:, tiles], std[:, tiles])
                root(t_small[:, 1, h * HB:(h + 1) * HB], t_small[:, 0, h * HB:(h + 1) * HB])
                act.wait_ge(affine_ready, h + 1)
                for b in range(HB):
                    bb = h * HB + b
                    src = zT_ps[h][:, b * S:(b + 1) * S]
                    nc.scalar.activation(h_full[:, bb, :], src, ACT.Identity, bias=shift_T[:, bb:bb + 1],
                                         scale=scale_T[:, bb:bb + 1]).then_inc(h_scaled, 1)
                    nc.scalar.activation(h_high[:, bb, :], src, ACT.Identity, bias=shift_T[:, bb:bb + 1],
                                         scale=scale_T[:, bb:bb + 1]).then_inc(h_scaled, 1)
                if h == 0:
                    for u in range(2):
                        relu_unit(act, 0, u)
            for u in range(2, UNITS):
                if u == 6:
                    act.wait_ge(logits_shifted, 1)
                    nc.scalar.activation(gt[:, 1, :, :], gt[:, 0, :, :], ACT.Exp).then_inc(exps_ready, 1)
                relu_unit(act, 0, u)
            with act.Fori(1, E) as e:
                for u in range(UNITS):
                    relu_unit(act, e, u)

        @block.tensor
        def _(pe):
            mm = nc.tensor.matmul

            def transpose_x(h):
                pe.wait_ge(x_loaded[h], 16)
                for j in range(HJ):
                    last = nc.tensor.transpose(xT_ps[h][:, j * P:(j + 1) * P], x_sb[:, h * HJ + j, :], ident[:, :])
                last.then_inc(xT_in_psum, 1)

            def down(h):
                pe.wait_ge(xT_ready, h + 1)
                for b in range(HB):
                    rows = slice((h * HB + b) * A, (h * HB + b + 1) * A)
                    last = mm(down_ps[rows, :], EARLY.of(early_sb, "down"), xT[:, h, b * S:(b + 1) * S],
                              start=True, stop=True, tile_position=(0, rows.start), skip_group_check=True)
                last.then_inc(down_in_psum, 1)

            def up(h):
                view = up_ps[h][:, :].rearrange("p (b t d) -> p b t d", b=HB, t=T)
                for b in range(HB):
                    for t in range(T):
                        mm(view[:, b, t, :], row_of[:, h * HB + b, :], bias_row[:, :],
                           start=(b == 0 and t == 0), stop=False, skip_group_check=True)
                if h == 0:
                    pe.wait_ge(up_diag_ready, 1)
                pe.wait_ge(gelu_ready, h + 1)
                rows = slice(h * HB * A, (h + 1) * HB * A)
                for t in range(T):
                    last = mm(view[:, :, t, :], hidden_T[rows, t * P:(t + 1) * P], up_diag[rows, :, :],
                              start=False, stop=True, skip_group_check=True)
                last.then_inc(up_in_psum, 1)

            def transpose_z(h):
                pe.wait_ge(z_ready, h + 1)
                for j in range(HJ):
                    last = nc.tensor.transpose(zT_ps[h][:, j * P:(j + 1) * P], z[:, h * HJ + j, :], ident[:, :])
                last.then_inc(zT_in_psum, 1)

            def router(h):
                for j in range(h * HJ, (h + 1) * HJ):
                    last = mm(logit_ps[:, j, :], h_full[:, j // T, (j % T) * P:(j % T + 1) * P],
                              STYLE.of(style_sb, "router"), start=True, stop=True, skip_group_check=True)
                last.then_inc(logits_in_psum, 1)

            def three(ps, w, moving_low, moving_high, first, last_):
                mm(ps, w_low[:, w], moving_high, start=first, stop=False)
                mm(ps, w_high[:, w], moving_low, start=False, stop=False)
                return mm(ps, w_high[:, w], moving_high, start=False, stop=last_)

            def first_product(e, u):
                unit, half, c = UNITS * e + u, u // FC, u % FC
                if u in (0, 2):
                    pe.wait_ge(w_low_ready, 4 * e + u // 2 + 1)
                moving = [t[:, half * HB:(half + 1) * HB, :].rearrange("p b s -> p (b s)") for t in (h_low, h_high)]
                three(hid_ps[u % RING][:, :], slice(c * P, (c + 1) * P), *moving, True, True).then_inc(hid_in_psum, 1)

            def second_product(e, u, before=0):
                unit, half, c = UNITS * e + u - UNITS * before, u // FC, u % FC
                if half == 0 and c in (0, 2):
                    pe.wait_ge(w_low_ready, 4 * e - 4 * before + 2 + c // 2 + 1)
                pe.wait_ge(hid_split, unit + 1)
                if c == 0 and not (isinstance(e, int) and e == 0):
                    pe.wait_ge(y_taken, HALVES * e - HALVES + half + 1)
                three(y_ps[half][:, :], slice(FF + c * P, FF + (c + 1) * P), hid_low[:, u % RING, :],
                      hid_high[:, u % RING, :], c == 0, c == FC - 1).then_inc(down_done, 1)

            pe.wait_ge(ident_ready, 1)
            transpose_x(0)
            pe.wait_ge(onehots_ready, 1)
            nc.tensor.transpose(pick_ps, onehot_x[:, :, :].rearrange("e b a -> e (b a)"), ident[0:DOMAINS, 0:DOMAINS]
                                ).then_inc(pick_in_psum, 1)
            transpose_x(1)
            pe.wait_ge(early_loaded, 16)
            down(0)
            pe.wait_ge(domain_loaded, 16)
            mm(bias_T_ps, DOMAIN.of(domain_sb, "expert_b", DOMAINS), onehot_v[:, :], start=True, stop=False)
            mm(bias_T_ps, DOMAIN.of(domain_sb, "emb", DOMAINS), onehot_d[:, :], start=False, stop=True
               ).then_inc(bias_T_in_psum, 1)
            down(1)
            pe.wait_ge(masks_ready, 5)
            pe.wait_ge(bias_T_ready, 1)
            mm(bias_row_ps, bias_T[:, :], DOMAIN.of(domain_sb, "up", A), start=True, stop=False)
            mm(bias_row_ps, ones[:, :], DOMAIN.of(domain_sb, "up_b", 1), start=False, stop=True
               ).then_inc(bias_row_in_psum, 1)
            pe.wait_ge(w_diag_ready, 1)
            mm(up_eff_ps, w_diag[:, :, :].rearrange("p b a -> p (b a)"), DOMAIN.of(domain_sb, "up"),
               start=True, stop=True).then_inc(up_eff_in_psum, 1)
            pe.wait_ge(style_loaded, 16)
            pe.wait_ge(bias_row_ready, 1)
            mm(se_ps, STYLE.of(style_sb, "subj", SUBJ), onehot_s[:, :], start=True, stop=True).then_inc(style_in_psum, 1)
            up(0)
            pe.wait_ge(style_ready, 1)
            mm(hyp1_ps, STYLE.of(style_sb, "hyp1", SE), se_T[:, :], start=True, stop=True).then_inc(style_in_psum, 1)
            up(1)
            pe.wait_ge(style_ready, 2)
            mm(hyp2_ps, STYLE.of(style_sb, "hyp2"), hyp1_T[:, :], start=True, stop=True).then_inc(style_in_psum, 1)
            pe.wait_ge(style_ready, 3)
            mm(sty1_ps, STYLE.of(style_sb, "sty1"), hyp2_T[:, :], start=True, stop=True).then_inc(style_in_psum, 1)
            pe.wait_ge(style_ready, 4)
            sty2 = STYLE.of(style_sb, "sty2", SC)
            mm(gam_ps, sty2[:, 0:D], sty1_T[:, :], start=True, stop=True).then_inc(style_in_psum, 1)
            mm(bet_ps, sty2[:, D:2 * D], sty1_T[:, :], start=True, stop=True).then_inc(style_in_psum, 1)
            transpose_z(0)
            pe.wait_ge(h_ready, 1)
            pe.wait_ge(up_taken, 2)
            for u in range(LEAD):
                first_product(0, u)
            router(0)
            first_product(0, 2)
            second_product(0, 0)
            first_product(0, 3)
            second_product(0, 1)
            transpose_z(1)
            pe.wait_ge(h_ready, 2)
            for u in range(4, UNITS):
                first_product(0, u)
                second_product(0, u - LEAD)
                if u == 4:
                    router(1)

            def expert(e):
                for u in range(UNITS):
                    first_product(e, u)
                    if u < LEAD:
                        second_product(e, UNITS - LEAD + u, before=1)
                    else:
                        second_product(e, u - LEAD)

            first_product(1, 0)
            second_product(1, UNITS - LEAD, before=1)
            pe.wait_ge(gates_ready, 1)
            for h in range(HALVES):
                for j in range(HJ):
                    last = nc.tensor.transpose((misc0, misc1)[h][0:E, j * P:(j + 1) * P], gates[:, h * HJ + j, :],
                                               ident[:, :])
                last.then_inc(gates_T_in_psum, 1)
            first_product(1, 1)
            second_product(1, UNITS - LEAD + 1, before=1)
            for u in range(LEAD, UNITS):
                first_product(1, u)
                second_product(1, u - LEAD)
            with pe.Fori(2, E) as e:
                expert(e)
            for u in range(LEAD):
                second_product(E, UNITS - LEAD + u, before=1)
            for h in range(HALVES):
                pe.wait_ge(y_added, HALVES * (E - 1) + h + 1)
                if h == 0:
                    pe.wait_ge(gates_T_ready, 2)
                for j in range(HJ):
                    last = nc.tensor.transpose((misc0, misc1)[h][:, j * P:(j + 1) * P],
                                               y_sum[:, h, j * P:(j + 1) * P], ident[:, :])
                last.then_inc(yT_in_psum, 1)

        @block.vector
        def _(ve):
            v = nc.vector
            steps = Count()

            def own():
                ve.wait_ge(vec_steps, steps.n)

            ve.wait_ge(ids_loaded, 16)
            v.tensor_copy(ids_f[:, :], ids_i[:, :]).then_inc(vec_steps, steps.add())
            own()
            dom, sub = ids_f[0:DOMAINS, 0:B], ids_f[:, B:2 * B]
            v.tensor_scalar(id_t[0:DOMAINS, 0, 0:B], dom, 0.0, None, ALU.is_ge).then_inc(vec_steps, steps.add())
            v.tensor_scalar(id_t[0:DOMAINS, 1, 0:B], dom, 0.0, float(DOMAINS - 1), ALU.max, ALU.min
                            ).then_inc(vec_steps, steps.add())
            v.tensor_scalar(id_t[:, 0, B:2 * B], sub, 0.0, float(SUBJ), ALU.is_lt, ALU.mult
                            ).then_inc(vec_steps, steps.add())
            own()
            v.scalar_tensor_tensor(id_t[0:DOMAINS, 2, 0:B], dom, float(DOMAINS), id_t[0:DOMAINS, 0, 0:B],
                                   ALU.is_lt, ALU.mult).then_inc(vec_steps, steps.add())
            v.tensor_tensor(id_t[:, 1, B:2 * B], sub, id_t[:, 0, B:2 * B], ALU.add).then_inc(vec_steps, steps.add())
            ve.wait_ge(masks_ready, 1)
            v.tensor_scalar(onehot_d[:, :], id_t[0:DOMAINS, 1, 0:B], lane[0:DOMAINS, :], None, ALU.is_equal
                            ).then_inc(vec_steps, steps.add())
            own()
            v.tensor_tensor(onehot_v[:, :], onehot_d[:, :], id_t[0:DOMAINS, 2, 0:B], ALU.mult
                            ).then_inc(vec_steps, steps.add())
            v.tensor_scalar(id_t[:, 2, B:2 * B], id_t[:, 1, B:2 * B], 0.0, float(SUBJ - 1), ALU.max, ALU.min
                            ).then_inc(vec_steps, steps.add())
            own()
            v.tensor_scalar(onehot_s[:, :], id_t[:, 2, B:2 * B], lane[0:SUBJ, :], None, ALU.is_equal
                            ).then_inc(vec_steps, steps.add())
            v.tensor_copy(onehot_x[:, :, :], onehot_v[:, :].unsqueeze(2).broadcast_to([DOMAINS, B, A])
                          ).then_inc(onehots_ready, 1)
            ve.wait_ge(masks_ready, 5)
            v.tensor_tensor(in_pair[:, :], in_sample[:, 0:HB], in_sample[:, HB:B], ALU.add).then_inc(vec_steps, steps.add())
            ve.wait_ge(ident_ready, 1)
            v.tensor_reduce(eye_a[:, :], ident[:, :].rearrange("p (b a) -> p a b", b=B), AX, ALU.add
                            ).then_inc(vec_steps, steps.add())

            ve.wait_ge(pick_in_psum, 1)
            v.tensor_copy(pick[:, :], pick_ps).then_inc(vec_steps, steps.add())
            own()
            ve.wait_ge(domain_loaded, 16)
            w4 = DOMAIN.of(domain_sb, "expert").rearrange("p (a e) -> p a e", e=DOMAINS)
            v.tensor_tensor(picked[:, :, :], w4, pick[:, :].unsqueeze(1).broadcast_to([P, A, DOMAINS]), ALU.mult
                            ).then_inc(vec_steps, steps.add())
            v.tensor_reduce(invalid[:, 0:1], pick[:, :], AX, ALU.add).then_inc(vec_steps, steps.add())
            own()
            v.tensor_reduce(w_sel[:, :], picked[:, :, :], AX, ALU.add).then_inc(vec_steps, steps.add())
            v.tensor_scalar(invalid[:, 1:2], invalid[:, 0:1], -1.0, 1.0, ALU.mult, ALU.add
                            ).then_inc(vec_steps, steps.add())
            own()
            v.scalar_tensor_tensor(w_eff[:, :], eye_a[:, :], invalid[:, 1:2], w_sel[:, :], ALU.mult, ALU.add
                                   ).then_inc(vec_steps, steps.add())
            own()
            v.tensor_tensor(w_diag[:, :, :], w_eff[:, :].unsqueeze(1).broadcast_to([P, B, A]),
                            in_sample[:, :].unsqueeze(2).broadcast_to([P, B, A]), ALU.mult).then_inc(w_diag_ready, 1)
            ve.wait_ge(bias_T_in_psum, 1)
            v.tensor_copy(bias_T[:, :], bias_T_ps).then_inc(bias_T_ready, 1)
            ve.wait_ge(bias_row_in_psum, 1)
            v.tensor_copy(bias_row[:, :], bias_row_ps).then_inc(bias_row_ready, 1)
            ve.wait_ge(up_eff_in_psum, 1)
            for b in range(HB):
                last = v.tensor_scalar(up_diag[:, b, :], up_eff_ps, in_pair[:, b:b + 1], None, ALU.mult)
                if b == HB - 1:
                    last.then_inc(up_diag_ready, 1)
                else:
                    last.then_inc(vec_steps, steps.add())

            roots = Count()

            def variance(j, dst, src, eps, k):
                for i in range(k):
                    v.bn_stats(stats[:, j + i, :], src(j + i)).then_inc(vec_steps, steps.add())
                own()
                for i in range(k):
                    v.bn_aggr(mv[:, j + i, :], stats[:, j + i, :]).then_inc(vec_steps, steps.add())
                own()
                v.tensor_scalar(dst, mv[:, j:j + k, 1], eps, None, ALU.add).then_inc(var_ready, 1)
                roots.add()
                ve.wait_ge(std_ready, roots.n)

            def adapter_norm(h):
                tiles = slice(h * HJ, (h + 1) * HJ)
                ve.wait_ge(up_in_psum, h + 1)
                v.tensor_tensor(res[:, tiles, :], up_ps[h][:, :].rearrange("p (j d) -> p j d", d=D), x_sb[:, tiles, :],
                                ALU.add).then_inc(up_taken, 1)
                ve.wait_ge(up_taken, h + 1)
                variance(h * HJ, std[:, tiles], lambda j: res[:, j, :], LN_EPS, HJ)
                v.reciprocal(rstd[:, tiles], std[:, tiles]).then_inc(vec_steps, steps.add())
                for j in range(h * HJ, (h + 1) * HJ):
                    v.scalar_tensor_tensor(res[:, j, :], res[:, j, :], mv[:, j, 0:1], ln0_sb[:, 0, :],
                                           ALU.subtract, ALU.mult).then_inc(vec_steps, steps.add())
                own()
                for j in range(h * HJ, (h + 1) * HJ):
                    v.scalar_tensor_tensor(x1[:, j, :], res[:, j, :], rstd[:, j:j + 1], ln0_sb[:, 1, :],
                                           ALU.mult, ALU.add).then_inc(vec_steps, steps.add())
                own()

            def token_norm(h):
                tiles = slice(h * HJ, (h + 1) * HJ)
                variance(h * HJ, std[:, tiles], lambda j: x1[:, j, :], LN_EPS, HJ)
                v.reciprocal(rstd[:, tiles], std[:, tiles]).then_inc(vec_steps, steps.add())
                own()
                for j in range(h * HJ, (h + 1) * HJ):
                    last = v.tensor_scalar(z[:, j, :], x1[:, j, :], mv[:, j, 0:1], rstd[:, j:j + 1],
                                           ALU.subtract, ALU.mult)
                    if j < (h + 1) * HJ - 1:
                        last.then_inc(vec_steps, steps.add())
                    else:
                        last.then_inc(z_ready, 1)

            def instance_norm(h):
                bs = slice(h * HB, (h + 1) * HB)
                ve.wait_ge(zT_in_psum, h + 1)
                for b in range(HB):
                    v.bn_stats(t_stats[:, h * HB + b, :], zT_ps[h][:, b * S:(b + 1) * S]).then_inc(vec_steps, steps.add())
                own()
                for b in range(h * HB, (h + 1) * HB):
                    v.bn_aggr(t_mv[:, b, :], t_stats[:, b, :]).then_inc(vec_steps, steps.add())
                own()
                v.tensor_scalar(t_small[:, 0, bs], t_mv[:, bs, 1], g2[:, 0:1], IN_EPS, ALU.mult, ALU.add
                                ).then_inc(var_ready, 1)
                v.tensor_scalar(t_small[:, 2, bs], t_mv[:, bs, 0], col(C_LNG), col(C_LNB), ALU.mult, ALU.add
                                ).then_inc(vec_steps, steps.add())
                own()
                v.tensor_scalar(t_small[:, 3, bs], t_small[:, 2, bs], -1.0, col(C_LNB), ALU.mult, ALU.add
                                ).then_inc(vec_steps, steps.add())
                roots.add()
                ve.wait_ge(std_ready, roots.n)
                v.reciprocal(t_small[:, 4, bs], t_small[:, 1, bs]).then_inc(vec_steps, steps.add())
                own()
                v.tensor_tensor(t_small[:, 5, bs], t_small[:, 4, bs], gamma_T[:, bs], ALU.mult
                                ).then_inc(vec_steps, steps.add())
                own()
                v.tensor_scalar(scale_T[:, bs], t_small[:, 5, bs], col(C_LNG), None, ALU.mult
                                ).then_inc(vec_steps, steps.add())
                v.tensor_tensor(t_small[:, 6, bs], t_small[:, 5, bs], t_small[:, 3, bs], ALU.mult
                                ).then_inc(vec_steps, steps.add())
                own()
                v.tensor_tensor(shift_T[:, bs], t_small[:, 6, bs], beta_T[:, bs], ALU.add).then_inc(affine_ready, 1)
                ve.wait_ge(h_scaled, 2 * HB * (h + 1))
                v.tensor_tensor(h_low[:, bs, :], h_full[:, bs, :], h_high[:, bs, :].bitcast(F32), ALU.subtract
                                ).then_inc(h_ready, 1)

            def style_network():
                ve.wait_ge(style_in_psum, 1)
                v.tensor_copy(se_T[:, :], se_ps).then_inc(style_ready, 1)
                ve.wait_ge(style_in_psum, 2)
                v.tensor_scalar(hyp1_T[:, :], hyp1_ps, col(C_HB1), 0.0, ALU.add, ALU.max).then_inc(style_ready, 1)
                ve.wait_ge(style_in_psum, 3)
                v.tensor_scalar(hyp2_T[:, :], hyp2_ps, col(C_HB2), None, ALU.add).then_inc(style_ready, 1)
                ve.wait_ge(style_in_psum, 4)
                v.tensor_scalar(sty1_T[:, :], sty1_ps, col(C_SB1, SC), 0.0, ALU.add, ALU.max).then_inc(style_ready, 1)
                ve.wait_ge(style_in_psum, 6)
                v.tensor_scalar(gamma_raw[:, :], gam_ps, col(C_SBG), None, ALU.add).then_inc(vec_steps, steps.add())
                v.tensor_scalar(beta_T[:, :], bet_ps, col(C_SBB), None, ALU.add).then_inc(vec_steps, steps.add())
                v.tensor_scalar(g2[:, :], col(C_LNG), col(C_LNG), None, ALU.mult).then_inc(vec_steps, steps.add())
                own()
                v.scalar_tensor_tensor(soft[:, 0, :], gamma_raw[:, :], -1.0, gamma_raw[:, :], ALU.mult, ALU.min
                                       ).then_inc(soft_in, 1)

            def softplus():
                ve.wait_ge(soft_ln, 1)
                v.scalar_tensor_tensor(gamma_T[:, :], gamma_raw[:, :], 0.0, soft[:, 2, :], ALU.max, ALU.add
                                       ).then_inc(vec_steps, steps.add())
                own()
                v.tensor_scalar(gamma_T[:, :], gamma_T[:, :], 1e-8, None, ALU.add).then_inc(vec_steps, steps.add())

            ve.wait_ge(early_loaded, 16)
            style_network()
            softplus()
            ve.wait_ge(ln0_loaded, 16)
            adapter_norm(0)
            token_norm(0)

            def round_weights(e, q):
                v.tensor_copy(w_high[:, quarter(q)], w_raw[:, e, quarter(q)]).then_inc(w_high_ready, 1)

            def split_hidden(e, u):
                unit, slot = UNITS * e + u, u % RING
                ve.wait_ge(hid_rounded, 2 * unit + 2)
                v.tensor_tensor(hid_low[:, slot, :], hid_full[:, slot, :], hid_high[:, slot, :].bitcast(F32),
                                ALU.subtract).then_inc(hid_split, 1)

            def take_expert(e, h):
                ve.wait_ge(down_done, UNITS * e + FC * (h + 1))
                ve.wait_ge(y_added, HALVES * e + h - 1)
                v.scalar_tensor_tensor(y_part[:, h, :], y_ps[h][:, :], cols[:, bass.ds(C_B2 + e, 1)],
                                       gate_all[:, bass.ds(e, 1), h * HN:(h + 1) * HN].rearrange("p a n -> p (a n)"),
                                       ALU.add, ALU.mult).then_inc(y_taken, 1)

            def take_first(h):
                ve.wait_ge(down_done, FC * (h + 1))
                v.tensor_scalar(y_part[:, h, :], y_ps[h][:, :], col(C_B2), None, ALU.add).then_inc(y_taken, 1)

            instance_norm(0)
            ve.wait_ge(w0_loaded, 16)
            for q in range(4):
                round_weights(0, q)

            adapter_norm(1)
            split_hidden(0, 0)
            token_norm(1)
            split_hidden(0, 1)
            instance_norm(1)
            split_hidden(0, 2)
            split_hidden(0, 3)

            def bc(a):
                return a.unsqueeze(2).broadcast_to([P, J, E])

            def g_shift():
                ve.wait_ge(logits_in_psum, 2)
                v.tensor_reduce(gs[:, 0, :], logit_ps, AX, ALU.max).then_inc(vec_steps, steps.add())
                own()
                v.tensor_tensor(gt[:, 0, :, :], logit_ps, bc(gs[:, 0, :]), ALU.subtract).then_inc(logits_shifted, 1)

            rank_b = rank[:, :].unsqueeze(1).broadcast_to([P, J, E])

            def g_probs():
                ve.wait_ge(exps_ready, 1)
                v.tensor_reduce(gs[:, 1, :], gt[:, 1, :, :], AX, ALU.add).then_inc(vec_steps, steps.add())
                own()
                v.reciprocal(gs[:, 2, :], gs[:, 1, :]).then_inc(vec_steps, steps.add())
                own()
                v.tensor_tensor(gt[:, 2, :, :], gt[:, 1, :, :], bc(gs[:, 2, :]), ALU.mult).then_inc(vec_steps, steps.add())
                own()

            def g_top(src, best, hit, at, onehot):
                v.tensor_reduce(best, src, AX, ALU.max).then_inc(vec_steps, steps.add())
                own()
                v.tensor_tensor(hit, src, bc(best), ALU.is_equal).then_inc(vec_steps, steps.add())
                own()
                v.tensor_tensor(hit, hit, rank_b, ALU.mult).then_inc(vec_steps, steps.add())
                own()
                v.tensor_reduce(at, hit, AX, ALU.max).then_inc(vec_steps, steps.add())
                own()
                v.tensor_tensor(onehot, rank_b, bc(at), ALU.is_equal).then_inc(vec_steps, steps.add())
                own()

            def g_first():
                g_top(gt[:, 2, :, :], gs[:, 3, :], gt[:, 3, :, :], gs[:, 4, :], gt[:, 4, :, :])
                v.scalar_tensor_tensor(gt[:, 5, :, :], gt[:, 4, :, :], -2.0, gt[:, 2, :, :], ALU.mult, ALU.add
                                       ).then_inc(vec_steps, steps.add())
                own()

            def g_second():
                g_top(gt[:, 5, :, :], gs[:, 5, :], gt[:, 6, :, :], gs[:, 6, :], gt[:, 7, :, :])

            def g_renorm():
                v.tensor_tensor(gs[:, 7, :], gs[:, 3, :], gs[:, 5, :], ALU.add).then_inc(vec_steps, steps.add())
                own()
                v.reciprocal(gs[:, 7, :], gs[:, 7, :]).then_inc(vec_steps, steps.add())
                own()
                v.tensor_tensor(gs[:, 8, :], gs[:, 3, :], gs[:, 7, :], ALU.mult).then_inc(vec_steps, steps.add())
                v.tensor_tensor(gs[:, 9, :], gs[:, 5, :], gs[:, 7, :], ALU.mult).then_inc(vec_steps, steps.add())
                own()
                v.tensor_tensor(gt[:, 4, :, :], gt[:, 4, :, :], bc(gs[:, 8, :]), ALU.mult).then_inc(vec_steps, steps.add())
                v.tensor_tensor(gt[:, 7, :, :], gt[:, 7, :, :], bc(gs[:, 9, :]), ALU.mult).then_inc(vec_steps, steps.add())
                own()
                v.tensor_tensor(gates[:, :, :], gt[:, 4, :, :], gt[:, 7, :, :], ALU.add).then_inc(gates_ready, 1)

            g_shift()
            split_hidden(0, 4)
            split_hidden(0, 5)
            take_first(0)
            ve.wait_ge(w_loaded, 16)
            ve.wait_ge(hid_in_psum, 6)
            round_weights(1, 0)
            g_probs()
            split_hidden(0, 6)
            g_first()
            split_hidden(0, 7)
            ve.wait_ge(hid_in_psum, UNITS)
            round_weights(1, 1)
            ve.wait_ge(down_done, 6)
            round_weights(1, 2)
            g_second()
            g_renorm()

            def expert(e, last=False, first=False):
                split_hidden(e, 0)
                split_hidden(e, 1)
                if first:
                    take_first(1)
                    for h in range(HALVES):
                        ve.wait_ge(gates_T_in_psum, h + 1)
                        v.tensor_copy(gates_T[:, h * HN:(h + 1) * HN], (misc0, misc1)[h][0:E, :]).then_inc(gates_T_ready, 1)
                else:
                    take_expert(e - 1, 1)
                round_weights_at(e, 3, down_done, UNITS * e)
                for u in range(2, 6):
                    split_hidden(e, u)
                if first:
                    ve.wait_ge(gate_loaded, 16)
                take_expert(e, 0)
                if not last:
                    round_weights_at(e + 1, 0, hid_in_psum, UNITS * e + 6)
                split_hidden(e, 6)
                split_hidden(e, 7)
                if not last:
                    round_weights_at(e + 1, 1, hid_in_psum, UNITS * e + 8)
                    round_weights_at(e + 1, 2, down_done, UNITS * e + 6)

            def round_weights_at(e, q, products, value):
                ve.wait_ge(w_loaded, 16)
                ve.wait_ge(products, value)
                v.tensor_copy(w_high[:, quarter(q)],
                              w_raw[:, bass.ds(e, 1), quarter(q)].rearrange("p a n -> p (a n)")).then_inc(w_high_ready, 1)

            expert(1, first=True)
            with ve.Fori(2, E - 1) as e:
                expert(e)
            expert(E - 1, last=True)
            take_expert(E - 1, 1)
            for h in range(HALVES):
                ve.wait_ge(yT_in_psum, h + 1)
                v.tensor_tensor(out_sb[:, h * HJ:(h + 1) * HJ, :], (misc0, misc1)[h][:, :].rearrange("p (j d) -> p j d", d=D),
                                x1[:, h * HJ:(h + 1) * HJ, :], ALU.add).then_inc(out_ready, 1)


def _padded(a):
    a = np.asarray(a)
    full = np.zeros((P,) + a.shape[1:], a.dtype)
    full[:a.shape[0]] = a
    return full


def _column(a):
    return _padded(np.reshape(a, (-1, 1)))


def kernel(x, itok_B_0_15, itok_B_6_14, L0_cond_down_W, L0_cond_down_b, L0_cond_up_W, L0_cond_up_b,
           L0_cond_expert_W, L0_cond_expert_b, L0_cond_domain_emb, L0_cond_ln_gamma, L0_cond_ln_beta,
           L1_cond_ln_g, L1_cond_ln_b, L1_cond_subj_emb, L1_cond_hyp_w1, L1_cond_hyp_b1, L1_cond_hyp_w2,
           L1_cond_hyp_b2, L1_cond_sty_w1, L1_cond_sty_b1, L1_cond_sty_w2, L1_cond_sty_b2, L1_cond_router_w,
           L1_cond_exp_w1, L1_cond_exp_b1, L1_cond_exp_w2, L1_cond_exp_b2):
    import concourse.bacc as bacc
    from concourse.bass_utils import run_bass_kernel_spmd

    f = {k: np.asarray(v) for k, v in dict(
        down=L0_cond_down_W, up=L0_cond_up_W, expert=L0_cond_expert_W, b1=L1_cond_exp_b1, w1=L1_cond_exp_w1,
        w2=L1_cond_exp_w2).items()}
    b1 = np.repeat(f["b1"].reshape(E, 1, FC, P), HALVES, axis=1).reshape(E * UNITS, P).T
    cols = np.concatenate([b1, np.asarray(L1_cond_exp_b2).T, _column(L1_cond_ln_g),
                           _column(L1_cond_ln_b), _column(L1_cond_hyp_b1), _column(L1_cond_hyp_b2),
                           _column(L1_cond_sty_b1), _column(L1_cond_sty_b2[:D]), _column(L1_cond_sty_b2[D:]),
                           np.tile(np.asarray(L0_cond_down_b), B).reshape(P, 1)], axis=1)
    early = np.concatenate([f["down"].T, cols], axis=1)
    expert = np.tile(f["expert"].transpose(1, 2, 0).reshape(A, A * DOMAINS), (B, 1))
    domain = np.concatenate([np.tile(f["up"].T, (B, 1)), expert, _padded(L0_cond_expert_b),
                             _padded(L0_cond_domain_emb), _padded(np.reshape(L0_cond_up_b, (1, D)))], axis=1)
    style = np.concatenate([_padded(L1_cond_subj_emb), _padded(L1_cond_hyp_w1), np.asarray(L1_cond_hyp_w2),
                            np.asarray(L1_cond_sty_w1), _padded(L1_cond_sty_w2), np.asarray(L1_cond_router_w)], axis=1)
    w_all = np.concatenate([f["w1"].transpose(1, 0, 2),
                            f["w2"].reshape(E, FC, P, D).transpose(2, 0, 1, 3).reshape(P, E, FF)], axis=2)
    arrays = {
        "x": np.asarray(x),
        "ids": np.concatenate([np.asarray(itok_B_0_15), np.asarray(itok_B_6_14)]).reshape(1, 2 * B),
        "early": early, "domain": domain, "style": style,
        "ln_row": np.stack([np.asarray(L0_cond_ln_gamma), np.asarray(L0_cond_ln_beta)]).reshape(1, 2, D),
        "w_all": w_all,
    }
    arrays = {k + "_dram": np.ascontiguousarray(v) for k, v in arrays.items()}
    nc = bacc.Bacc("TRN2", target_bir_lowering=False, num_devices=1)
    args = [nc.dram_tensor(k, v.shape, mybir.dt.from_np(v.dtype), kind="ExternalInput").ap()
            for k, v in arrays.items()]
    args.append(nc.dram_tensor("out_dram", (B, S, D), F32, kind="ExternalOutput").ap())
    adapter_moe(nc, *args)
    result = run_bass_kernel_spmd(nc, [arrays], core_ids=[0])
    return result.results[0]["out_dram"]
```

```python
from contextlib import ExitStack

import numpy as np

import concourse.bass as bass
from concourse import mybir

F32 = mybir.dt.float32
F32R = mybir.dt.float32r
I32 = mybir.dt.int32
ALU = mybir.AluOpType
ACT = mybir.ActivationFunctionType
AX = mybir.AxisListType.X

P = 128
B, S, D = 4, 256, 128
N = B * S
T = S // P
J = B * T
HALVES = 2
HN = N // HALVES
HB = B // HALVES
HJ = J // HALVES
A, DOMAINS = 32, 16
E, FF = 8, 512
FC = FF // P
SUBJ, SE, SH, SC = 32, 64, 128, 64
UNITS = HALVES * FC
RING = 4
LEAD = 2
PRE_ORDER = [(0, 0), (1, 0), (0, 1), (1, 1)]
PRE_BLOCKS, PRE_UNITS = len(PRE_ORDER), len(PRE_ORDER) * FC
LN_EPS, IN_EPS = 1e-5, 1e-8

C_B1, C_B2 = 0, E * UNITS
C_LNG, C_LNB, C_HB1, C_HB2, C_SB1, C_SBG, C_SBB, C_DB = range(C_B2 + E, C_B2 + E + 8)
COLS = C_DB + 1
AUG = A + 1
GROUPS = A + 2
SLOT = 64


class Packed:

    def __init__(self, **widths):
        self.at, self.width = {}, 0
        for name, width in widths.items():
            self.at[name] = (self.width, self.width + width)
            self.width += width

    def of(self, tile, name, rows=P):
        a, b = self.at[name]
        return tile[0:rows, a:b]


EARLY = Packed(down=A, cols=COLS, up=D, up_b=D)
STYLE = Packed(subj=SE, hyp1=SH, hyp2=SH, sty1=SC, sty2=2 * D, router=E)


class Count:

    def __init__(self):
        self.n = 0

    def add(self, k=1):
        self.n += k
        return k


def adapter_moe(nc, xT, ids, tables, early, style, ln_row, w_all, out):
    ctx = ExitStack()
    with ctx:
        def sb(name, shape, dt=F32):
            return ctx.enter_context(nc.sbuf_tensor(name, shape, dt))

        def sem(name):
            return ctx.enter_context(nc.semaphore(name))

        xT_sb = sb("xT_sb", [P, N])
        tables_sb = sb("tables_sb", [P, GROUPS, DOMAINS])
        early_sb = sb("early_sb", [P, EARLY.width])
        style_sb = sb("style_sb", [P, STYLE.width])
        ln0_sb = sb("ln0_sb", [P, 2, D])
        ids_i = sb("ids_i", [P, 1 + B], I32)
        ident = sb("ident", [P, P])
        lane = sb("lane", [P, 1])
        domain_no = sb("domain_no", [P, DOMAINS])
        rank = sb("rank", [P, E])
        in_sample = sb("in_sample", [P, B])
        eye_a = sb("eye_a", [P, A])
        ids_f = sb("ids_f", [P, 1 + B])
        dom = sb("dom", [P, 4])
        subj = sb("subj", [SUBJ, 3, B])
        onehot_s = sb("onehot_s", [SUBJ, B])
        pick = sb("pick", [P, 2, DOMAINS])
        picked = sb("picked", [P, GROUPS, DOMAINS])
        w_sel = sb("w_sel", [P, GROUPS])
        w_eff = sb("w_eff", [P, AUG])
        w_diag = sb("w_diag", [P, B, SLOT])
        up_eff = sb("up_eff", [P, HALVES, D])
        hidden = sb("hidden", [P, HALVES, S])
        se_T = sb("se_T", [SE, B])
        hyp1_T = sb("hyp1_T", [SH, B])
        hyp2_T = sb("hyp2_T", [SH, B])
        sty1_T = sb("sty1_T", [SC, B])
        gamma_raw = sb("gamma_raw", [P, B])
        beta_T = sb("beta_T", [P, B])
        soft = sb("soft", [P, 3, B])
        gamma_T = sb("gamma_T", [P, B])
        gamma_g = sb("gamma_g", [P, B])
        g2 = sb("g2", [P, 1])
        centred = sb("centred", [P, J, D])
        x1 = sb("x1", [P, J, D])
        stats = sb("stats", [P, 2, J, 6])
        mv = sb("mv", [P, 2, J, 2])
        std = sb("std", [P, 2, J])
        rstd = sb("rstd", [P, 2, J])
        z_shift = sb("z_shift", [P, J])
        z = sb("z", [P, J, D])
        t_stats = sb("t_stats", [P, B, 6])
        t_mv = sb("t_mv", [P, B, 2])
        t_var = sb("t_var", [P, B])
        t_std = sb("t_std", [P, B])
        t_rstd = sb("t_rstd", [P, B])
        t_mean = sb("t_mean", [P, B])
        t_off = sb("t_off", [P, B])
        scale_T = sb("scale_T", [P, B])
        shift_T = sb("shift_T", [P, B])
        h_full = sb("h_full", [P, B, S])
        h_high = sb("h_high", [P, B, S], F32R)
        h_low = sb("h_low", [P, B, S], F32R)
        gt = sb("gt", [P, 8, J, E])
        gs = sb("gs", [P, 10, J])
        gates = sb("gates", [P, J, E])
        gates_T = sb("gates_T", [E, N])
        gate_all = sb("gate_all", [P, E, N])
        w_raw = sb("w_raw", [P, E, 2 * FF])
        w_high = [sb(f"w_high{k}", [P, 2 * FF], F32R) for k in range(2)]
        w_low = [sb(f"w_low{k}", [P, 2 * FF], F32R) for k in range(2)]
        hid_full = sb("hid_full", [P, RING, HN])
        hid_high = sb("hid_high", [P, RING, HN], F32R)
        hid_low = sb("hid_low", [P, RING, HN], F32R)
        y_raw = sb("y_raw", [P, PRE_BLOCKS, HN])
        y_gated = sb("y_gated", [P, HN])
        y_part = sb("y_part", [P, HALVES, HN])
        y_sum = sb("y_sum", [P, HALVES, HN])
        out_sb = sb("out_sb", [P, J, D])
        scratch = nc.dram_tensor("gate_scratch", [E, N], F32, kind="Internal").ap()

        bank = [ctx.enter_context(nc.psum_tensor(f"bank{i}", [P, 512], F32)) for i in range(8)]
        hid_ps = bank[0:RING]
        y_ps = bank[4:6]
        misc = bank[6:8]
        sum_ps = [bank[i][:, 0:T * D].rearrange("p (t d) -> p t d", d=D) for i in (0, 1, 6, 7)]
        down_ps = bank[2:4]
        up_eff_ps = bank[4][:, 0:HALVES * D]
        zT_ps = [bank[i][:, 0:S] for i in (4, 5, 6, 7)]
        se_ps, hyp1_ps, hyp2_ps, sty1_ps, gam_ps, bet_ps = (
            bank[5][0:r, c:c + B] for r, c in ((SE, 0), (SH, 8), (SH, 16), (SC, 24), (P, 32), (P, 40)))
        logit_ps = misc[0][:, 0:J * E].rearrange("p (j e) -> p j e", e=E)

        cols = EARLY.of(early_sb, "cols")

        def col(c, rows=P):
            return cols[0:rows, c:c + 1]

        x_loaded = [sem(f"x_loaded{h}") for h in range(HALVES)]
        ids_loaded, tables_loaded, early_loaded = sem("ids_loaded"), sem("tables_loaded"), sem("early_loaded")
        style_loaded, ln0_loaded = sem("style_loaded"), sem("ln0_loaded")
        w_loaded = [sem("w0_loaded"), sem("w1_loaded"), sem("w_loaded")]
        pool_steps = sem("pool_steps")
        ident_ready, masks_ready, ones_ready = sem("ident_ready"), sem("masks_ready"), sem("ones_ready")
        vec_steps = sem("vec_steps")
        onehots_ready = sem("onehots_ready")
        w_diag_ready, up_eff_in_psum, up_eff_ready = sem("w_diag_ready"), sem("up_eff_in_psum"), sem("up_eff_ready")
        down_in_psum, gelu_ready, sum_in_psum = sem("down_in_psum"), sem("gelu_ready"), sem("sum_in_psum")
        style_in_psum, style_ready = sem("style_in_psum"), sem("style_ready")
        soft_in, soft_exp, soft_ln = sem("soft_in"), sem("soft_exp"), sem("soft_ln")
        sum_taken = sem("sum_taken")
        var_ready, std_ready = sem("var_ready"), sem("std_ready")
        z_affine, z_ready, zT_in_psum = sem("z_affine"), sem("z_ready"), sem("zT_in_psum")
        affine_ready, h_rounded, h_ready = sem("affine_ready"), sem("h_rounded"), sem("h_ready")
        h_full_ready = sem("h_full_ready")
        logits_in_psum, logits_shifted, exps_ready = sem("logits_in_psum"), sem("logits_shifted"), sem("exps_ready")
        gates_ready, gates_T_in_psum, gates_T_ready = sem("gates_ready"), sem("gates_T_in_psum"), sem("gates_T_ready")
        gates_stored, gate01_loaded, gate_loaded = sem("gates_stored"), sem("gate01_loaded"), sem("gate_loaded")
        w_high_ready, w_low_ready = sem("w_high_ready"), sem("w_low_ready")
        hid_in_psum = sem("hid_in_psum")
        hid_relu = sem("hid_relu")
        hid_round = sem("hid_round")
        hid_split = sem("hid_split")
        down_done = sem("down_done")
        y_taken, y_added = sem("y_taken"), sem("y_added")
        y_gated_ready = sem("y_gated_ready")
        yT_in_psum, out_ready, out_stored = sem("yT_in_psum"), sem("out_ready"), sem("out_stored")

        out_dram = out.rearrange("b (t p) d -> p (b t) d", p=P)

        block = ctx.enter_context(nc.Block())

        def quarter(q):
            return slice(q * 256, (q + 1) * 256)

        def w_set(e):
            return 1 if isinstance(e, int) and e == 1 else 0

        @block.sync
        def _(sp):
            sp.dma_start(ids_i[:, :], ids).then_inc(ids_loaded, 16)
            sp.dma_start(xT_sb[:, 0:HN], xT[:, 0:HN]).then_inc(x_loaded[0], 16)
            sp.dma_start(xT_sb[:, HN:N], xT[:, HN:N]).then_inc(x_loaded[1], 16)
            sp.dma_start(ln0_sb[:, :, :], ln_row.rearrange("a b d -> a (b d)")[0, :].partition_broadcast(P)
                         ).then_inc(ln0_loaded, 16)
            for e in range(2):
                sp.dma_start(w_raw[:, e, :], w_all[:, e, :]).then_inc(w_loaded[e], 16)
            sp.dma_start(w_raw[:, 2:E, :], w_all[:, 2:E, :]).then_inc(w_loaded[2], 16)
            sp.wait_ge(gates_T_ready, 2)
            sp.dma_start(scratch, gates_T[:, :]).then_inc(gates_stored, 16)
            sp.wait_ge(gates_stored, 16)
            sp.dma_start(gate_all[:, 0:2, :], scratch[0:2, :].rearrange("e n -> (e n)").partition_broadcast(P)
                         ).then_inc(gate01_loaded, 16)
            sp.dma_start(gate_all[:, 2:E, :], scratch[2:E, :].rearrange("e n -> (e n)").partition_broadcast(P)
                         ).then_inc(gate_loaded, 16)
            for b in range(B):
                sp.wait_ge(out_ready, b + 1)
                sp.dma_start(out_dram[:, b * T:(b + 1) * T, :], out_sb[:, b * T:(b + 1) * T, :]).then_inc(out_stored, 16)
            sp.wait_ge(out_stored, 16 * B)

        @block.gpsimd
        def _(pool):
            steps = Count()

            def split_low(e, q):
                pool.wait_ge(w_high_ready, 4 * e + q + 1)
                nc.gpsimd.tensor_tensor(w_low[w_set(e)][:, quarter(q)], w_raw[:, e, quarter(q)],
                                        w_high[w_set(e)][:, quarter(q)].bitcast(F32), ALU.subtract
                                        ).then_inc(w_low_ready, 1)

            def add_block(e, h):
                pool.wait_ge(y_taken, HALVES * e + h + 1)
                nc.gpsimd.tensor_tensor(y_sum[:, h, :], y_sum[:, h, :], y_part[:, h, :], ALU.add).then_inc(y_added, 1)

            nc.gpsimd.memset(ident[:, :], 0.0).then_inc(pool_steps, steps.add())
            nc.gpsimd.iota(domain_no[:, :], pattern=[[1, DOMAINS]], base=0, channel_multiplier=0,
                           allow_small_or_imprecise_dtypes=True).then_inc(masks_ready, 1)
            pool.wait_ge(pool_steps, steps.n)
            nc.gpsimd.affine_select(out=ident[:, :], in_=ident[:, :], compare_op=ALU.not_equal, fill=1.0,
                                    base=0, pattern=[[-1, P]], channel_multiplier=1).then_inc(ident_ready, 1)
            nc.gpsimd.iota(lane[:, :], pattern=[[0, 1]], base=0, channel_multiplier=1,
                           allow_small_or_imprecise_dtypes=True).then_inc(masks_ready, 1)
            nc.gpsimd.memset(in_sample[:, :], 1.0).then_inc(pool_steps, steps.add())
            nc.gpsimd.memset(w_diag[:, :, :], 0.0).then_inc(masks_ready, 1)
            pool.wait_ge(pool_steps, steps.n)
            nc.gpsimd.affine_select(out=in_sample[:, :], in_=in_sample[:, :], compare_op=ALU.is_ge, fill=0.0,
                                    base=0, pattern=[[-A, B]], channel_multiplier=1).then_inc(pool_steps, steps.add())
            pool.wait_ge(pool_steps, steps.n)
            nc.gpsimd.affine_select(out=in_sample[:, :], in_=in_sample[:, :], compare_op=ALU.is_ge, fill=0.0,
                                    base=A - 1, pattern=[[A, B]], channel_multiplier=-1).then_inc(masks_ready, 1)
            nc.gpsimd.iota(rank[:, :], pattern=[[-1, E]], base=E, channel_multiplier=0,
                           allow_small_or_imprecise_dtypes=True).then_inc(masks_ready, 1)

            for e in range(2):
                for q in range(4):
                    split_low(e, q)
            for q in range(3):
                split_low(2, q)
            pool.wait_ge(gate01_loaded, 16)
            for k, (e, h) in enumerate(PRE_ORDER):
                pool.wait_ge(y_taken, k + 1)
                gate = gate_all[:, e, h * HN:(h + 1) * HN]
                if e == 0:
                    nc.gpsimd.tensor_tensor(y_sum[:, h, :], y_raw[:, k, :], gate, ALU.mult).then_inc(y_added, 1)
                else:
                    pool.wait_ge(y_added, k)
                    nc.gpsimd.tensor_tensor(y_gated[:, :], y_raw[:, k, :], gate, ALU.mult).then_inc(y_gated_ready, 1)
                    pool.wait_ge(y_gated_ready, h + 1)
                    nc.gpsimd.tensor_tensor(y_sum[:, h, :], y_sum[:, h, :], y_gated[:, :], ALU.add).then_inc(y_added, 1)

            def expert(e, last=False):
                split_low(e, 3)
                if not (isinstance(e, int) and e == 2):
                    add_block(e - 1, 1)
                if not last:
                    split_low(e + 1, 0)
                    add_block(e, 0)
                    split_low(e + 1, 1)
                    split_low(e + 1, 2)

            expert(2)
            with pool.Fori(3, E - 1) as e:
                expert(e)
            expert(E - 1, last=True)

        @block.scalar
        def _(act):
            ac = nc.scalar.activation
            act.dma_start(tables_sb[:, :, :], tables).then_inc(tables_loaded, 16)
            act.dma_start(early_sb[:, :], early).then_inc(early_loaded, 16)
            act.dma_start(style_sb[:, :], style).then_inc(style_loaded, 16)
            nc.scalar.preload_act_table(ACT.Gelu)
            act.wait_ge(early_loaded, 16)
            for b in range(B):
                rows = slice((b % HB) * SLOT, (b % HB) * SLOT + A)
                act.wait_ge(down_in_psum, b + 1)
                ac(hidden[rows, b // HB, :], down_ps[b // HB][rows, 0:S], ACT.Gelu,
                   bias=cols[rows, C_DB:C_DB + 1]).then_inc(gelu_ready, 1)
            nc.scalar.preload_act_table_set("natural_log_exp_and_others")
            act.wait_ge(soft_in, 1)
            ac(soft[:, 1, :], soft[:, 0, :], ACT.Exp).then_inc(soft_exp, 1)
            act.wait_ge(soft_exp, 1)
            ac(soft[:, 2, :], soft[:, 1, :], ACT.Ln, bias=1.0).then_inc(soft_ln, 1)
            nc.scalar.preload_act_table(ACT.Sqrt)
            roots, zs = Count(), Count()

            def root(dst, src):
                roots.add()
                act.wait_ge(var_ready, roots.n)
                ac(dst, src, ACT.Sqrt).then_inc(std_ready, 1)

            def token_root(k, b):
                root(std[:, k, b * T:(b + 1) * T], std[:, k, b * T:(b + 1) * T])

            def feature_root(b):
                root(t_std[:, b:b + 1], t_var[:, b:b + 1])

            def normalise(b):
                act.wait_ge(z_affine, b + 1)
                for j in range(b * T, (b + 1) * T):
                    ac(z[:, j, :], x1[:, j, :], ACT.Identity, bias=z_shift[:, j:j + 1],
                       scale=rstd[:, 1, j:j + 1]).then_inc(z_ready, 1)

            def round_h(b):
                act.wait_ge(affine_ready, b + 1)
                ac(h_high[:, b, :], zT_ps[b], ACT.Identity, bias=shift_T[:, b:b + 1],
                   scale=scale_T[:, b:b + 1]).then_inc(h_rounded, 1)

            def round_first_weights(e):
                act.wait_ge(w_loaded[e], 16)
                for q in range(4):
                    ac(w_high[e][:, quarter(q)], w_raw[:, e, quarter(q)], ACT.Copy).then_inc(w_high_ready, 1)

            def relu_unit(e, u, q=None):
                q = UNITS * e + u if q is None else q
                slot = u % RING
                act.wait_ge(hid_in_psum, q + 1)
                bias = cols[:, bass.ds(C_B1 + e * UNITS + u, 1)]
                ac(hid_full[:, slot, :], hid_ps[slot][:, :], ACT.Relu, bias=bias).then_inc(hid_relu, 1)
                if u % 2 == 0:
                    ac(hid_high[:, slot, :], hid_ps[slot][:, :], ACT.Relu, bias=bias).then_inc(hid_relu, 1)

            def relu_pre(q):
                e, h = PRE_ORDER[q // FC]
                relu_unit(e, h * FC + q % FC, q)

            token_root(0, 0)
            token_root(0, 1)
            token_root(1, 0)
            token_root(1, 1)
            normalise(0)
            normalise(1)
            round_first_weights(0)
            token_root(0, 2)
            token_root(0, 3)
            feature_root(0)
            feature_root(1)
            round_h(0)
            round_h(1)
            round_first_weights(1)
            token_root(1, 2)
            token_root(1, 3)
            relu_pre(0)
            normalise(2)
            relu_pre(1)
            normalise(3)
            relu_pre(2)
            relu_pre(3)
            feature_root(2)
            feature_root(3)
            relu_pre(4)
            round_h(2)
            round_h(3)
            for q in range(5, 10):
                relu_pre(q)
            act.wait_ge(logits_shifted, 1)
            ac(gt[:, 1, :, :], gt[:, 0, :, :], ACT.Exp).then_inc(exps_ready, 1)
            for q in range(10, PRE_UNITS):
                relu_pre(q)
            with act.Fori(2, E) as e:
                for u in range(UNITS):
                    relu_unit(e, u)

        @block.tensor
        def _(pe):
            mm = nc.tensor.matmul

            def down(b):
                if b % HB == 0:
                    pe.wait_ge(x_loaded[b // HB], 16)
                row = (b % HB) * SLOT
                mm(down_ps[b // HB][row:row + A, 0:S], EARLY.of(early_sb, "down"), xT_sb[:, b * S:(b + 1) * S],
                   start=True, stop=True, tile_position=(0, row)).then_inc(down_in_psum, 1)

            def residual(b):
                for t in range(T):
                    mm(sum_ps[b][:, t, :], xT_sb[:, (b * T + t) * P:(b * T + t + 1) * P], ident[:, :],
                       start=(t == 0), stop=False, skip_group_check=True)

            def up(b):
                pe.wait_ge(gelu_ready, b + 1)
                row = (b % HB) * SLOT
                for t in range(T):
                    last = mm(sum_ps[b][:, t, :], hidden[row:row + AUG, b // HB, t * P:(t + 1) * P],
                              up_eff[row:row + AUG, b // HB, :], start=False, stop=True, skip_group_check=True)
                last.then_inc(sum_in_psum, 1)

            def transpose_z(b):
                pe.wait_ge(z_ready, T * (b + 1))
                for t in range(T):
                    last = nc.tensor.transpose(zT_ps[b][:, t * P:(t + 1) * P], z[:, b * T + t, :], ident[:, :])
                last.then_inc(zT_in_psum, 1)

            def router():
                for j in range(J):
                    last = mm(logit_ps[:, j, :], h_full[:, j // T, (j % T) * P:(j % T + 1) * P],
                              STYLE.of(style_sb, "router"), start=True, stop=True, skip_group_check=True)
                last.then_inc(logits_in_psum, 1)

            def three(ps, k, w, moving_low, moving_high, first, last_):
                mm(ps, w_low[k][:, w], moving_high, start=first, stop=False)
                mm(ps, w_high[k][:, w], moving_low, start=False, stop=False)
                return mm(ps, w_high[k][:, w], moving_high, start=False, stop=last_)

            def first_product(e, u):
                half, c = u // FC, u % FC
                if u in (0, 2):
                    pe.wait_ge(w_low_ready, 4 * e + u // 2 + 1)
                moving = [t[:, half * HB:(half + 1) * HB, :].rearrange("p b s -> p (b s)") for t in (h_low, h_high)]
                three(hid_ps[u % RING][:, :], w_set(e), slice(c * P, (c + 1) * P), *moving, True, True
                      ).then_inc(hid_in_psum, 1)

            def second_product(e, u, q, blk):
                half, c = u // FC, u % FC
                if half == 0 and c in (0, 2):
                    pe.wait_ge(w_low_ready, 4 * e + 2 + c // 2 + 1)
                pe.wait_ge(hid_split, q + 1)
                if c == 0 and not (isinstance(blk, int) and blk < 2):
                    pe.wait_ge(y_taken, blk - 1)
                three(y_ps[blk_parity(blk, u)][:, :], w_set(e), slice(FF + c * P, FF + (c + 1) * P),
                      hid_low[:, u % RING, :], hid_high[:, u % RING, :], c == 0, c == FC - 1).then_inc(down_done, 1)

            def blk_parity(blk, u):
                return blk % 2 if isinstance(blk, int) else u // FC

            def pre_first(q):
                e, h = PRE_ORDER[q // FC]
                first_product(e, h * FC + q % FC)

            def pre_second(q):
                e, h = PRE_ORDER[q // FC]
                second_product(e, h * FC + q % FC, q, q // FC)

            pe.wait_ge(ident_ready, 1)
            pe.wait_ge(early_loaded, 16)
            down(0)
            down(1)
            residual(0)
            residual(1)
            pe.wait_ge(w_diag_ready, 1)
            for b in range(B):
                row = (b % HB) * SLOT
                last = mm(up_eff_ps[row:row + SLOT, (b // HB) * D:(b // HB + 1) * D], w_diag[:, b, :],
                          EARLY.of(early_sb, "up"), start=True, stop=True, tile_position=(0, row),
                          skip_group_check=True)
            last.then_inc(up_eff_in_psum, 1)
            down(2)
            down(3)
            pe.wait_ge(style_loaded, 16)
            pe.wait_ge(onehots_ready, 1)
            mm(se_ps, STYLE.of(style_sb, "subj", SUBJ), onehot_s[:, :], start=True, stop=True).then_inc(style_in_psum, 1)
            pe.wait_ge(ones_ready, HB)
            pe.wait_ge(up_eff_ready, 1)
            up(0)
            up(1)
            pe.wait_ge(style_ready, 1)
            mm(hyp1_ps, STYLE.of(style_sb, "hyp1", SE), se_T[:, :], start=True, stop=True).then_inc(style_in_psum, 1)
            residual(2)
            pe.wait_ge(style_ready, 2)
            mm(hyp2_ps, STYLE.of(style_sb, "hyp2"), hyp1_T[:, :], start=True, stop=True).then_inc(style_in_psum, 1)
            residual(3)
            pe.wait_ge(style_ready, 3)
            mm(sty1_ps, STYLE.of(style_sb, "sty1"), hyp2_T[:, :], start=True, stop=True).then_inc(style_in_psum, 1)
            up(2)
            pe.wait_ge(style_ready, 4)
            sty2 = STYLE.of(style_sb, "sty2", SC)
            mm(gam_ps, sty2[:, 0:D], sty1_T[:, :], start=True, stop=True).then_inc(style_in_psum, 1)
            mm(bet_ps, sty2[:, D:2 * D], sty1_T[:, :], start=True, stop=True).then_inc(style_in_psum, 1)
            up(3)
            transpose_z(0)
            pe.wait_ge(soft_in, 1)
            transpose_z(1)
            pe.wait_ge(h_ready, 1)
            pre_first(0)
            pre_first(1)
            pre_first(2)
            pre_second(0)
            pre_first(3)
            transpose_z(2)
            pre_second(1)
            transpose_z(3)
            for q in range(4, 8):
                pre_first(q)
                pre_second(q - LEAD)
            pe.wait_ge(h_ready, 2)
            for q in range(8, 14):
                pre_first(q)
                pre_second(q - LEAD)
                if q == 8:
                    router()
            pre_first(14)
            pe.wait_ge(gates_ready, 1)
            for h in range(HALVES):
                for j in range(HJ):
                    last = nc.tensor.transpose(misc[1 - h][0:E, j * P:(j + 1) * P], gates[:, h * HJ + j, :], ident[:, :])
                last.then_inc(gates_T_in_psum, 1)
            pre_second(12)
            pre_first(15)
            pre_second(13)

            def expert(e):
                for u in range(UNITS):
                    first_product(e, u)
                    back = u < LEAD
                    second_product(e - back, (u - LEAD) % UNITS, UNITS * e + u - LEAD,
                                   HALVES * e - 1 if back else HALVES * e + (u - LEAD) // FC)

            def expert_two():
                for u in range(UNITS):
                    first_product(2, u)
                    if u < LEAD:
                        pre_second(PRE_UNITS - LEAD + u)
                    else:
                        second_product(2, u - LEAD, PRE_UNITS + u - LEAD, PRE_BLOCKS + (u - LEAD) // FC)

            expert_two()
            with pe.Fori(3, E) as e:
                expert(e)
            for u in range(UNITS - LEAD, UNITS):
                second_product(E - 1, u, UNITS * (E - 1) + u, HALVES * E - 1)
            pe.wait_ge(gates_T_ready, 2)
            for h in range(HALVES):
                pe.wait_ge(y_added, HALVES * (E - 2) + h + 1)
                for j in range(HJ):
                    mm(misc[h][:, j * P:(j + 1) * P], y_sum[:, h, j * P:(j + 1) * P], ident[:, :],
                       start=(j == 0), stop=False, skip_group_check=True)
                pe.wait_ge(y_taken, HALVES * (E - 1) + h + 1)
                for j in range(HJ):
                    last = mm(misc[h][:, j * P:(j + 1) * P], y_part[:, h, j * P:(j + 1) * P], ident[:, :],
                              start=False, stop=True, skip_group_check=True)
                last.then_inc(yT_in_psum, 1)

        @block.vector
        def _(ve):
            v = nc.vector
            steps = Count()

            def own():
                ve.wait_ge(vec_steps, steps.n)

            for b in range(HB):
                v.memset(hidden[b * SLOT + A:b * SLOT + A + 1, :, :], 1.0).then_inc(ones_ready, 1)
            ve.wait_ge(ids_loaded, 16)
            v.tensor_copy(ids_f[:, :], ids_i[:, :]).then_inc(vec_steps, steps.add())
            own()
            v.tensor_scalar(dom[:, 0:1], ids_f[:, 0:1], 0.0, None, ALU.is_ge).then_inc(vec_steps, steps.add())
            v.tensor_scalar(dom[:, 1:2], ids_f[:, 0:1], 0.0, float(DOMAINS - 1), ALU.max, ALU.min
                            ).then_inc(vec_steps, steps.add())
            v.tensor_scalar(subj[:, 0, :], ids_f[0:SUBJ, 1:1 + B], 0.0, float(SUBJ), ALU.is_lt, ALU.mult
                            ).then_inc(vec_steps, steps.add())
            own()
            v.scalar_tensor_tensor(dom[:, 2:3], ids_f[:, 0:1], float(DOMAINS), dom[:, 0:1], ALU.is_lt, ALU.mult
                                   ).then_inc(vec_steps, steps.add())
            ve.wait_ge(masks_ready, 2)
            v.tensor_scalar(pick[:, 0, :], domain_no[:, :], dom[:, 1:2], None, ALU.is_equal
                            ).then_inc(vec_steps, steps.add())
            v.tensor_tensor(subj[:, 1, :], subj[:, 0, :], ids_f[0:SUBJ, 1:1 + B], ALU.add).then_inc(vec_steps, steps.add())
            own()
            v.tensor_scalar(pick[:, 1, :], pick[:, 0, :], dom[:, 2:3], None, ALU.mult).then_inc(vec_steps, steps.add())
            v.tensor_scalar(dom[:, 3:4], dom[:, 2:3], -1.0, 1.0, ALU.mult, ALU.add).then_inc(vec_steps, steps.add())
            v.tensor_scalar(subj[:, 2, :], subj[:, 1, :], 0.0, float(SUBJ - 1), ALU.max, ALU.min
                            ).then_inc(vec_steps, steps.add())
            ve.wait_ge(ident_ready, 1)
            v.tensor_reduce(eye_a[:, :], ident[:, :].rearrange("p (b a) -> p a b", b=B), AX, ALU.add
                            ).then_inc(vec_steps, steps.add())
            own()
            v.tensor_scalar(onehot_s[:, :], subj[:, 2, :], lane[0:SUBJ, :], None, ALU.is_equal).then_inc(onehots_ready, 1)

            ve.wait_ge(tables_loaded, 16)
            v.tensor_tensor(picked[:, 0:AUG, :], tables_sb[:, 0:AUG, :],
                            pick[:, 1, :].unsqueeze(1).broadcast_to([P, AUG, DOMAINS]), ALU.mult
                            ).then_inc(vec_steps, steps.add())
            v.tensor_tensor(picked[:, AUG, :], tables_sb[:, AUG, :], pick[:, 0, :], ALU.mult
                            ).then_inc(vec_steps, steps.add())
            own()
            v.tensor_reduce(w_sel[:, :], picked[:, :, :], AX, ALU.add).then_inc(vec_steps, steps.add())
            own()
            v.scalar_tensor_tensor(w_eff[:, 0:A], eye_a[:, :], dom[:, 3:4], w_sel[:, 0:A], ALU.mult, ALU.add
                                   ).then_inc(vec_steps, steps.add())
            v.tensor_tensor(w_eff[:, A:AUG], w_sel[:, A:AUG], w_sel[:, AUG:GROUPS], ALU.add
                            ).then_inc(vec_steps, steps.add())
            ve.wait_ge(masks_ready, 4)
            own()
            v.tensor_tensor(w_diag[:, :, 0:AUG], w_eff[:, :].unsqueeze(1).broadcast_to([P, B, AUG]),
                            in_sample[:, :].unsqueeze(2).broadcast_to([P, B, AUG]), ALU.mult).then_inc(w_diag_ready, 1)
            ve.wait_ge(up_eff_in_psum, 1)
            v.tensor_tensor(up_eff[:, :, :], up_eff_ps.rearrange("p (h d) -> p h d", d=D),
                            EARLY.of(early_sb, "up_b").unsqueeze(1).broadcast_to([P, HALVES, D]), ALU.add
                            ).then_inc(up_eff_ready, 1)

            ve.wait_ge(style_in_psum, 1)
            v.tensor_copy(se_T[:, :], se_ps).then_inc(style_ready, 1)
            ve.wait_ge(style_in_psum, 2)
            v.tensor_scalar(hyp1_T[:, :], hyp1_ps, col(C_HB1), 0.0, ALU.add, ALU.max).then_inc(style_ready, 1)
            ve.wait_ge(style_in_psum, 3)
            v.tensor_scalar(hyp2_T[:, :], hyp2_ps, col(C_HB2), None, ALU.add).then_inc(style_ready, 1)
            ve.wait_ge(style_in_psum, 4)
            v.tensor_scalar(sty1_T[:, :], sty1_ps, col(C_SB1, SC), 0.0, ALU.add, ALU.max).then_inc(style_ready, 1)
            ve.wait_ge(style_in_psum, 6)
            v.tensor_scalar(gamma_raw[:, :], gam_ps, col(C_SBG), None, ALU.add).then_inc(vec_steps, steps.add())
            v.tensor_scalar(beta_T[:, :], bet_ps, col(C_SBB), None, ALU.add).then_inc(vec_steps, steps.add())
            v.tensor_scalar(g2[:, :], col(C_LNG), col(C_LNG), None, ALU.mult).then_inc(vec_steps, steps.add())
            own()
            v.scalar_tensor_tensor(soft[:, 0, :], gamma_raw[:, :], -1.0, gamma_raw[:, :], ALU.mult, ALU.min
                                   ).then_inc(soft_in, 1)

            def softplus():
                ve.wait_ge(soft_ln, 1)
                v.scalar_tensor_tensor(gamma_T[:, :], gamma_raw[:, :], 0.0, soft[:, 2, :], ALU.max, ALU.add
                                       ).then_inc(vec_steps, steps.add())
                own()
                v.tensor_scalar(gamma_T[:, :], gamma_T[:, :], 1e-8, None, ALU.add).then_inc(vec_steps, steps.add())
                own()
                v.tensor_scalar(gamma_g[:, :], gamma_T[:, :], col(C_LNG), None, ALU.mult).then_inc(vec_steps, steps.add())

            asked = Count()
            root_of = {}

            def token_stats(k, b, src):
                for t in range(T):
                    v.bn_stats(stats[:, k, b * T + t, :], src(t)).then_inc(vec_steps, steps.add())
                own()
                for j in range(b * T, (b + 1) * T):
                    v.bn_aggr(mv[:, k, j, :], stats[:, k, j, :]).then_inc(vec_steps, steps.add())
                own()
                asked.add()
                root_of[k, b] = asked.n
                v.tensor_scalar(std[:, k, b * T:(b + 1) * T], mv[:, k, b * T:(b + 1) * T, 1], LN_EPS, None, ALU.add
                                ).then_inc(var_ready, 1)

            def first_stats(b):
                ve.wait_ge(sum_in_psum, b + 1)
                token_stats(0, b, lambda t: sum_ps[b][:, t, :])

            def adapter_norm(b):
                ve.wait_ge(std_ready, root_of[0, b])
                v.reciprocal(rstd[:, 0, b * T:(b + 1) * T], std[:, 0, b * T:(b + 1) * T]).then_inc(vec_steps, steps.add())
                for t in range(T):
                    v.scalar_tensor_tensor(centred[:, b * T + t, :], sum_ps[b][:, t, :], mv[:, 0, b * T + t, 0:1],
                                           ln0_sb[:, 0, :], ALU.subtract, ALU.mult).then_inc(sum_taken, 1)
                own()
                for j in range(b * T, (b + 1) * T):
                    ve.wait_ge(sum_taken, j + 1)
                    v.scalar_tensor_tensor(x1[:, j, :], centred[:, j, :], rstd[:, 0, j:j + 1], ln0_sb[:, 1, :],
                                           ALU.mult, ALU.add).then_inc(vec_steps, steps.add())
                own()
                token_stats(1, b, lambda t: x1[:, b * T + t, :])

            def token_affine(b):
                ve.wait_ge(std_ready, root_of[1, b])
                js = slice(b * T, (b + 1) * T)
                v.reciprocal(rstd[:, 1, js], std[:, 1, js]).then_inc(vec_steps, steps.add())
                own()
                v.scalar_tensor_tensor(z_shift[:, js], mv[:, 1, js, 0], -1.0, rstd[:, 1, js], ALU.mult, ALU.mult
                                       ).then_inc(z_affine, 1)

            def feature_stats(b):
                one = slice(b, b + 1)
                ve.wait_ge(zT_in_psum, b + 1)
                v.bn_stats(t_stats[:, b, :], zT_ps[b]).then_inc(vec_steps, steps.add())
                own()
                v.bn_aggr(t_mv[:, b, :], t_stats[:, b, :]).then_inc(vec_steps, steps.add())
                own()
                asked.add()
                root_of[2, b] = asked.n
                v.tensor_scalar(t_var[:, one], t_mv[:, b, 1:2], g2[:, 0:1], IN_EPS, ALU.mult, ALU.add
                                ).then_inc(var_ready, 1)
                v.tensor_scalar(t_mean[:, one], t_mv[:, b, 0:1], col(C_LNG), col(C_LNB), ALU.mult, ALU.add
                                ).then_inc(vec_steps, steps.add())
                own()
                v.tensor_scalar(t_off[:, one], t_mean[:, one], -1.0, col(C_LNB), ALU.mult, ALU.add
                                ).then_inc(vec_steps, steps.add())
                own()
                v.tensor_tensor(t_off[:, one], t_off[:, one], gamma_T[:, one], ALU.mult).then_inc(vec_steps, steps.add())

            def feature_affine(b):
                one = slice(b, b + 1)
                ve.wait_ge(std_ready, root_of[2, b])
                v.reciprocal(t_rstd[:, one], t_std[:, one]).then_inc(vec_steps, steps.add())
                own()
                v.tensor_scalar(scale_T[:, one], gamma_g[:, one], t_rstd[:, one], None, ALU.mult
                                ).then_inc(vec_steps, steps.add())
                v.tensor_scalar(shift_T[:, one], t_off[:, one], t_rstd[:, one], beta_T[:, one], ALU.mult, ALU.add
                                ).then_inc(vec_steps, steps.add())
                ve.wait_ge(vec_steps, steps.n)
                ve.sem_inc(affine_ready, 1)

            def full_h(b):
                ve.wait_ge(h_rounded, b + 1)
                v.tensor_scalar(h_full[:, b, :], zT_ps[b], scale_T[:, b:b + 1], shift_T[:, b:b + 1], ALU.mult, ALU.add
                                ).then_inc(h_full_ready, 1)

            def low_h(b):
                ve.wait_ge(h_full_ready, b + 1)
                last = v.tensor_tensor(h_low[:, b, :], h_full[:, b, :], h_high[:, b, :].bitcast(F32), ALU.subtract)
                if b % HB == HB - 1:
                    last.then_inc(h_ready, 1)
                else:
                    last.then_inc(vec_steps, steps.add())

            def round_weights(e, q, products, value):
                ve.wait_ge(w_loaded[2], 16)
                ve.wait_ge(products, value)
                v.tensor_copy(w_high[0][:, quarter(q)],
                              w_raw[:, bass.ds(e, 1), quarter(q)].rearrange("p a n -> p (a n)")).then_inc(w_high_ready, 1)

            def split_hidden(u, q, relus, rounds):
                slot = u % RING
                ve.wait_ge(hid_relu, relus)
                if u % 2 == 1:
                    v.tensor_copy(hid_high[:, slot, :], hid_full[:, slot, :]).then_inc(hid_round, 1)
                    ve.wait_ge(hid_round, rounds)
                v.tensor_tensor(hid_low[:, slot, :], hid_full[:, slot, :], hid_high[:, slot, :].bitcast(F32),
                                ALU.subtract).then_inc(hid_split, 1)

            def split_pre(q):
                split_hidden(q, q, q // 2 * 3 + 2 + q % 2, q // 2 + 1)

            def split_loop(e, u):
                split_hidden(u, UNITS * e + u, UNITS // 2 * 3 * e + u // 2 * 3 + 2 + u % 2,
                             UNITS // 2 * e + u // 2 + 1)

            def take_pre(k):
                ve.wait_ge(down_done, FC * (k + 1))
                v.tensor_scalar(y_raw[:, k, :], y_ps[k % 2][:, :], col(C_B2 + PRE_ORDER[k][0]), None, ALU.add
                                ).then_inc(y_taken, 1)

            def take_block(e, h):
                ve.wait_ge(down_done, UNITS * e + FC * (h + 1))
                ve.wait_ge(y_added, HALVES * e + h - 1)
                v.scalar_tensor_tensor(y_part[:, h, :], y_ps[h][:, :], cols[:, bass.ds(C_B2 + e, 1)],
                                       gate_all[:, bass.ds(e, 1), h * HN:(h + 1) * HN].rearrange("p a n -> p (a n)"),
                                       ALU.add, ALU.mult).then_inc(y_taken, 1)

            first_stats(0)
            first_stats(1)
            ve.wait_ge(ln0_loaded, 16)
            adapter_norm(0)
            adapter_norm(1)
            token_affine(0)
            token_affine(1)
            softplus()
            first_stats(2)
            first_stats(3)
            feature_stats(0)
            feature_stats(1)
            feature_affine(0)
            feature_affine(1)
            full_h(0)
            full_h(1)
            low_h(0)
            low_h(1)
            adapter_norm(2)
            adapter_norm(3)
            split_pre(0)
            token_affine(2)
            split_pre(1)
            token_affine(3)
            split_pre(2)
            split_pre(3)
            feature_stats(2)
            feature_stats(3)
            feature_affine(2)
            feature_affine(3)
            split_pre(4)
            take_pre(0)
            full_h(2)
            full_h(3)
            low_h(2)
            low_h(3)
            split_pre(5)
            split_pre(6)
            split_pre(7)
            split_pre(8)

            def bc(a):
                return a.unsqueeze(2).broadcast_to([P, J, E])

            rank_b = rank[:, :].unsqueeze(1).broadcast_to([P, J, E])

            def g_shift():
                ve.wait_ge(logits_in_psum, 1)
                v.tensor_reduce(gs[:, 0, :], logit_ps, AX, ALU.max).then_inc(vec_steps, steps.add())
                own()
                v.tensor_tensor(gt[:, 0, :, :], logit_ps, bc(gs[:, 0, :]), ALU.subtract).then_inc(logits_shifted, 1)

            def g_probs():
                ve.wait_ge(exps_ready, 1)
                v.tensor_reduce(gs[:, 1, :], gt[:, 1, :, :], AX, ALU.add).then_inc(vec_steps, steps.add())
                own()
                v.reciprocal(gs[:, 2, :], gs[:, 1, :]).then_inc(vec_steps, steps.add())
                own()
                v.tensor_tensor(gt[:, 2, :, :], gt[:, 1, :, :], bc(gs[:, 2, :]), ALU.mult).then_inc(vec_steps, steps.add())
                own()

            def g_top(src, best, hit, at, onehot):
                v.tensor_reduce(best, src, AX, ALU.max).then_inc(vec_steps, steps.add())
                own()
                v.tensor_tensor(hit, src, bc(best), ALU.is_equal).then_inc(vec_steps, steps.add())
                own()
                v.tensor_tensor(hit, hit, rank_b, ALU.mult).then_inc(vec_steps, steps.add())
                own()
                v.tensor_reduce(at, hit, AX, ALU.max).then_inc(vec_steps, steps.add())
                own()
                v.tensor_tensor(onehot, rank_b, bc(at), ALU.is_equal).then_inc(vec_steps, steps.add())
                own()

            def g_first():
                g_top(gt[:, 2, :, :], gs[:, 3, :], gt[:, 3, :, :], gs[:, 4, :], gt[:, 4, :, :])
                v.scalar_tensor_tensor(gt[:, 5, :, :], gt[:, 4, :, :], -2.0, gt[:, 2, :, :], ALU.mult, ALU.add
                                       ).then_inc(vec_steps, steps.add())
                own()

            def g_second():
                g_top(gt[:, 5, :, :], gs[:, 5, :], gt[:, 6, :, :], gs[:, 6, :], gt[:, 7, :, :])

            def g_renorm():
                v.tensor_tensor(gs[:, 7, :], gs[:, 3, :], gs[:, 5, :], ALU.add).then_inc(vec_steps, steps.add())
                own()
                v.reciprocal(gs[:, 7, :], gs[:, 7, :]).then_inc(vec_steps, steps.add())
                own()
                v.tensor_tensor(gs[:, 8, :], gs[:, 3, :], gs[:, 7, :], ALU.mult).then_inc(vec_steps, steps.add())
                v.tensor_tensor(gs[:, 9, :], gs[:, 5, :], gs[:, 7, :], ALU.mult).then_inc(vec_steps, steps.add())
                own()
                v.tensor_tensor(gt[:, 4, :, :], gt[:, 4, :, :], bc(gs[:, 8, :]), ALU.mult).then_inc(vec_steps, steps.add())
                v.tensor_tensor(gt[:, 7, :, :], gt[:, 7, :, :], bc(gs[:, 9, :]), ALU.mult).then_inc(vec_steps, steps.add())
                own()
                v.tensor_tensor(gates[:, :, :], gt[:, 4, :, :], gt[:, 7, :, :], ALU.add).then_inc(gates_ready, 1)

            g_shift()
            take_pre(1)
            split_pre(9)
            g_probs()
            split_pre(10)
            g_first()
            split_pre(11)
            g_second()
            split_pre(12)
            g_renorm()
            take_pre(2)
            split_pre(13)
            for q in range(2):
                round_weights(2, q, hid_in_psum, 12)
            split_pre(14)
            for h in range(HALVES):
                ve.wait_ge(gates_T_in_psum, h + 1)
                v.tensor_copy(gates_T[:, h * HN:(h + 1) * HN], misc[1 - h][0:E, :]).then_inc(gates_T_ready, 1)
            round_weights(2, 2, down_done, 12)
            split_pre(15)

            def expert(e, last=False, first=False):
                split_loop(e, 0)
                split_loop(e, 1)
                round_weights(e, 3, down_done, UNITS * e - (4 if first else 0))
                if first:
                    take_pre(3)
                else:
                    take_block(e - 1, 1)
                for u in range(2, 5):
                    split_loop(e, u)
                if not last:
                    round_weights(e + 1, 0, hid_in_psum, UNITS * e + 6)
                split_loop(e, 5)
                if first:
                    ve.wait_ge(gate_loaded, 16)
                take_block(e, 0)
                split_loop(e, 6)
                if not last:
                    round_weights(e + 1, 1, hid_in_psum, UNITS * e + 8)
                split_loop(e, 7)
                if not last:
                    round_weights(e + 1, 2, down_done, UNITS * e + 6)

            expert(2, first=True)
            with ve.Fori(3, E - 1) as e:
                expert(e)
            expert(E - 1, last=True)
            take_block(E - 1, 1)
            for h in range(HALVES):
                ve.wait_ge(yT_in_psum, h + 1)
                for b in range(h * HB, (h + 1) * HB):
                    v.tensor_tensor(out_sb[:, b * T:(b + 1) * T, :],
                                    misc[h][:, (b % HB) * S:(b % HB + 1) * S].rearrange("p (t d) -> p t d", d=D),
                                    x1[:, b * T:(b + 1) * T, :], ALU.add).then_inc(out_ready, 1)


def _padded(a):
    a = np.asarray(a)
    full = np.zeros((P,) + a.shape[1:], a.dtype)
    full[:a.shape[0]] = a
    return full


def _column(a):
    return _padded(np.reshape(a, (-1, 1)))


def _slots(a):
    full = np.zeros((HB, SLOT), np.asarray(a).dtype)
    full[:, :A] = np.asarray(a)
    return full.reshape(P, 1)


def kernel(x, itok_B_0_15, itok_B_6_14, L0_cond_down_W, L0_cond_down_b, L0_cond_up_W, L0_cond_up_b,
           L0_cond_expert_W, L0_cond_expert_b, L0_cond_domain_emb, L0_cond_ln_gamma, L0_cond_ln_beta,
           L1_cond_ln_g, L1_cond_ln_b, L1_cond_subj_emb, L1_cond_hyp_w1, L1_cond_hyp_b1, L1_cond_hyp_w2,
           L1_cond_hyp_b2, L1_cond_sty_w1, L1_cond_sty_b1, L1_cond_sty_w2, L1_cond_sty_b2, L1_cond_router_w,
           L1_cond_exp_w1, L1_cond_exp_b1, L1_cond_exp_w2, L1_cond_exp_b2):
    import concourse.bacc as bacc
    from concourse.bass_utils import run_bass_kernel_spmd

    f = {k: np.asarray(v) for k, v in dict(
        down=L0_cond_down_W, up=L0_cond_up_W, expert=L0_cond_expert_W, b1=L1_cond_exp_b1, w1=L1_cond_exp_w1,
        w2=L1_cond_exp_w2).items()}
    b1 = np.repeat(f["b1"].reshape(E, 1, FC, P), HALVES, axis=1).reshape(E * UNITS, P).T
    cols = np.concatenate([b1, np.asarray(L1_cond_exp_b2).T, _column(L1_cond_ln_g),
                           _column(L1_cond_ln_b), _column(L1_cond_hyp_b1), _column(L1_cond_hyp_b2),
                           _column(L1_cond_sty_b1), _column(L1_cond_sty_b2[:D]), _column(L1_cond_sty_b2[D:]),
                           _slots(L0_cond_down_b)], axis=1)
    up_b = np.zeros((P, D), f["up"].dtype)
    up_b[A::SLOT] = np.asarray(L0_cond_up_b)
    early = np.concatenate([f["down"].T, cols, np.tile(f["up"].T, (B, 1)), up_b], axis=1)
    tables = np.concatenate([f["expert"].transpose(1, 2, 0), np.asarray(L0_cond_expert_b).T[:, None, :],
                             np.asarray(L0_cond_domain_emb).T[:, None, :]], axis=1)
    tables = np.tile(tables, (B, 1, 1))
    ids = np.concatenate([np.repeat(np.asarray(itok_B_0_15), A).reshape(P, 1),
                          np.tile(np.asarray(itok_B_6_14), (P, 1))], axis=1)
    style = np.concatenate([_padded(L1_cond_subj_emb), _padded(L1_cond_hyp_w1), np.asarray(L1_cond_hyp_w2),
                            np.asarray(L1_cond_sty_w1), _padded(L1_cond_sty_w2), np.asarray(L1_cond_router_w)], axis=1)
    w_all = np.concatenate([f["w1"].transpose(1, 0, 2),
                            f["w2"].reshape(E, FC, P, D).transpose(2, 0, 1, 3).reshape(P, E, FF)], axis=2)
    arrays = {
        "xT": np.asarray(x).reshape(N, D).T,
        "ids": ids, "tables": tables, "early": early, "style": style,
        "ln_row": np.stack([np.asarray(L0_cond_ln_gamma), np.asarray(L0_cond_ln_beta)]).reshape(1, 2, D),
        "w_all": w_all,
    }
    arrays = {k + "_dram": np.ascontiguousarray(v) for k, v in arrays.items()}
    nc = bacc.Bacc("TRN2", target_bir_lowering=False, num_devices=1)
    args = [nc.dram_tensor(k, v.shape, mybir.dt.from_np(v.dtype), kind="ExternalInput").ap()
            for k, v in arrays.items()]
    args.append(nc.dram_tensor("out_dram", (B, S, D), F32, kind="ExternalOutput").ap())
    adapter_moe(nc, *args)
    result = run_bass_kernel_spmd(nc, [arrays], core_ids=[0])
    return result.results[0]["out_dram"]
```

```python
from contextlib import ExitStack

import numpy as np

import concourse.bass as bass
from concourse import mybir

F32 = mybir.dt.float32
F32R = mybir.dt.float32r
I32 = mybir.dt.int32
ALU = mybir.AluOpType
ACT = mybir.ActivationFunctionType
AX = mybir.AxisListType.X

P = 128
B, S, D = 4, 256, 128
N = B * S
T = S // P
J = B * T
HALVES = 2
HN = N // HALVES
HB = B // HALVES
HJ = J // HALVES
A, DOMAINS = 32, 16
E, FF = 8, 512
FC = FF // P
SUBJ, SE, SH, SC = 32, 64, 128, 64
UNITS = HALVES * FC
RING = 4
LEAD = 3
PRE_ORDER = [(0, 0), (1, 0), (0, 1), (1, 1), (2, 0), (2, 1)]
EARLY_HIGHS = (1, 3, 5)
POOL_SPLITS = (0, 2, 3, 4, 5, 6, 8, 10, 12, 14, 16, 18, 20, 22)
WARM_LOAD, WARM_NORM = 9, (3, 8)
PRE_BLOCKS, PRE_UNITS = len(PRE_ORDER), len(PRE_ORDER) * FC
LN_EPS, IN_EPS = 1e-5, 1e-8

C_B1, C_B2 = 0, E * UNITS
C_LNG, C_LNB, C_HB1, C_HB2, C_SB1, C_SBG, C_SBB, C_DB = range(C_B2 + E, C_B2 + E + 8)
COLS = C_DB + 1
AUG = A + 1
GROUPS = A + 2
SLOT = 64


class Packed:

    def __init__(self, **widths):
        self.at, self.width = {}, 0
        for name, width in widths.items():
            self.at[name] = (self.width, self.width + width)
            self.width += width

    def of(self, tile, name, rows=P):
        a, b = self.at[name]
        return tile[0:rows, a:b]


EARLY = Packed(down=A, cols=COLS, up=D, up_b=D)
STYLE = Packed(subj=SE, hyp1=SH, hyp2=SH, sty1=SC, sty2=2 * D, router=E)


class Count:

    def __init__(self):
        self.n = 0

    def add(self, k=1):
        self.n += k
        return k


def adapter_moe(nc, xT, ids, tables, early, style, ln_row, w_all, out):
    ctx = ExitStack()
    with ctx:
        def sb(name, shape, dt=F32):
            return ctx.enter_context(nc.sbuf_tensor(name, shape, dt))

        def sem(name):
            return ctx.enter_context(nc.semaphore(name))

        xT_sb = sb("xT_sb", [P, N])
        tables_sb = sb("tables_sb", [P, GROUPS, DOMAINS])
        early_sb = sb("early_sb", [P, EARLY.width])
        style_sb = sb("style_sb", [P, STYLE.width])
        ln0_sb = sb("ln0_sb", [P, 2, D])
        ids_i = sb("ids_i", [P, 1 + B], I32)
        ident = sb("ident", [P, P])
        lane = sb("lane", [P, 1])
        domain_no = sb("domain_no", [P, DOMAINS])
        rank = sb("rank", [P, E])
        in_sample = sb("in_sample", [P, B])
        eye_a = sb("eye_a", [P, A])
        ids_f = sb("ids_f", [P, 1 + B])
        dom = sb("dom", [P, 4])
        subj = sb("subj", [SUBJ, 3, B])
        onehot_s = sb("onehot_s", [SUBJ, B])
        pick = sb("pick", [P, 2, DOMAINS])
        picked = sb("picked", [P, GROUPS, DOMAINS])
        w_sel = sb("w_sel", [P, GROUPS])
        w_eff = sb("w_eff", [P, AUG])
        w_diag = sb("w_diag", [P, B, SLOT])
        up_eff = sb("up_eff", [P, HALVES, D])
        hidden = sb("hidden", [P, HALVES, S])
        se_T = sb("se_T", [SE, B])
        hyp1_T = sb("hyp1_T", [SH, B])
        hyp2_T = sb("hyp2_T", [SH, B])
        sty1_T = sb("sty1_T", [SC, B])
        gamma_raw = sb("gamma_raw", [P, B])
        beta_T = sb("beta_T", [P, B])
        soft = sb("soft", [P, 3, B])
        gamma_T = sb("gamma_T", [P, B])
        gamma_g = sb("gamma_g", [P, B])
        g2 = sb("g2", [P, 1])
        centred = sb("centred", [P, J, D])
        x1 = sb("x1", [P, J, D])
        stats = sb("stats", [P, 2, J, 6])
        mv = sb("mv", [P, 2, J, 2])
        std = sb("std", [P, 2, J])
        eps = sb("eps", [P, 2])
        rstd = sb("rstd", [P, 2, J])
        z_shift = sb("z_shift", [P, J])
        z = sb("z", [P, J, D])
        t_stats = sb("t_stats", [P, B, 6])
        t_mv = sb("t_mv", [P, B, 2])
        t_std = sb("t_std", [P, B])
        t_rstd = sb("t_rstd", [P, B])
        t_gain = sb("t_gain", [P, B])
        t_off = sb("t_off", [P, B])
        scale_T = sb("scale_T", [P, B])
        shift_T = sb("shift_T", [P, B])
        h_full = sb("h_full", [P, B, S])
        h_high = sb("h_high", [P, B, S], F32R)
        h_low = sb("h_low", [P, B, S], F32R)
        gt = sb("gt", [P, 8, J, E])
        gs = sb("gs", [P, 10, J])
        gates = sb("gates", [P, E, J])
        gates_T = sb("gates_T", [E * J, P])
        gate_all = sb("gate_all", [P, E, N])
        w_raw = sb("w_raw", [P, E, 2 * FF])
        w_high = [sb(f"w_high{k}", [P, 2 * FF], F32R) for k in range(2)]
        w_low = [sb(f"w_low{k}", [P, 2 * FF], F32R) for k in range(2)]
        hid_full = sb("hid_full", [P, RING, HN])
        hid_high = sb("hid_high", [P, RING, HN], F32R)
        hid_low = sb("hid_low", [P, RING, HN], F32R)
        y_raw = sb("y_raw", [P, PRE_BLOCKS, HN])
        y_gated = sb("y_gated", [P, HN])
        y_part = sb("y_part", [P, HALVES, HN])
        y_sum = sb("y_sum", [P, HALVES, HN])
        out_sb = sb("out_sb", [P, J, D])
        scratch = nc.dram_tensor("gate_scratch", [E, N], F32, kind="Internal").ap()

        bank = [ctx.enter_context(nc.psum_tensor(f"bank{i}", [P, 512], F32)) for i in range(8)]
        hid_ps = bank[0:RING]
        y_ps = bank[4:6]
        misc = bank[6:8]
        sum_last = [misc[1], bank[0]]
        sum_ps = [bank[i][:, 0:T * D].rearrange("p (t d) -> p t d", d=D) for i in (0, 1, 6, 7)]
        down_ps = bank[2:4]
        up_eff_ps = bank[4][:, 0:HALVES * D]
        zT_ps = [bank[i][:, 0:S] for i in (4, 5, 6, 7)]
        se_ps, hyp1_ps, hyp2_ps, sty1_ps, gam_ps, bet_ps = (
            bank[5][0:r, c:c + B] for r, c in ((SE, 0), (SH, 8), (SH, 16), (SC, 24), (P, 32), (P, 40)))
        logit_ps = misc[0][:, S:S + J * E].rearrange("p (j e) -> p j e", e=E)

        cols = EARLY.of(early_sb, "cols")

        def col(c, rows=P):
            return cols[0:rows, c:c + 1]

        x_loaded = [sem(f"x_loaded{h}") for h in range(HALVES)]
        ids_loaded, tables_loaded, early_loaded = sem("ids_loaded"), sem("tables_loaded"), sem("early_loaded")
        style_loaded, ln0_loaded = sem("style_loaded"), sem("ln0_loaded")
        w_loaded = [sem("w0_loaded"), sem("w1_loaded"), sem("w_loaded")]
        pool_steps = sem("pool_steps")
        ident_ready, masks_ready, ones_ready = sem("ident_ready"), sem("masks_ready"), sem("ones_ready")
        vec_steps = sem("vec_steps")
        onehots_ready = sem("onehots_ready")
        w_diag_ready, up_eff_in_psum, up_eff_ready = sem("w_diag_ready"), sem("up_eff_in_psum"), sem("up_eff_ready")
        down_in_psum, gelu_ready, sum_in_psum = sem("down_in_psum"), sem("gelu_ready"), sem("sum_in_psum")
        style_in_psum, style_ready = sem("style_in_psum"), sem("style_ready")
        gamma_beta_ready = sem("gamma_beta_ready")
        soft_in, soft_exp, soft_ln = sem("soft_in"), sem("soft_exp"), sem("soft_ln")
        sum_taken = sem("sum_taken")
        var_ready, std_ready = sem("var_ready"), sem("std_ready")
        z_affine, z_ready, zT_in_psum = sem("z_affine"), sem("z_ready"), sem("zT_in_psum")
        z_odd_ready = sem("z_odd_ready")
        affine_ready, h_rounded, h_ready = sem("affine_ready"), sem("h_rounded"), sem("h_ready")
        h_full_ready = sem("h_full_ready")
        logits_in_psum, logits_shifted, exps_ready = sem("logits_in_psum"), sem("logits_shifted"), sem("exps_ready")
        gates_ready, gates_T_in_psum, gates_T_ready = sem("gates_ready"), sem("gates_T_in_psum"), sem("gates_T_ready")
        gates_stored = sem("gates_stored")
        gate_loaded = [sem(f"gate{e}_loaded") for e in range(5)]
        w_high_ready, w_low_ready = sem("w_high_ready"), sem("w_low_ready")
        hid_in_psum = sem("hid_in_psum")
        hid_relu = sem("hid_relu")
        hid_round = sem("hid_round")
        hid_split = sem("hid_split")
        hid_split_pool = sem("hid_split_pool")
        down_done = sem("down_done")
        y_taken, y_added = sem("y_taken"), sem("y_added")
        y_gated_ready, first_added = sem("y_gated_ready"), sem("first_added")
        eps_ready = sem("eps_ready")
        yT_in_psum, out_ready, out_stored = sem("yT_in_psum"), sem("out_ready"), sem("out_stored")

        out_dram = out.rearrange("b (t p) d -> p (b t) d", p=P)

        block = ctx.enter_context(nc.Block())

        def quarter(q):
            return slice(q * 256, (q + 1) * 256)

        def w_set(e):
            return 1 if isinstance(e, int) and e == 1 else 0

        def relus_of(q):
            return q + 1 + sum(scalar_high(i) for i in range(q + 1))

        def rounds_of(q):
            return sum(not scalar_high(i) for i in range(q + 1))

        def scalar_high(q):
            return q % 2 == 0 or q in EARLY_HIGHS

        def is_pool(q):
            return q in POOL_SPLITS

        @block.sync
        def _(sp):
            sp.dma_start(ids_i[:, :], ids).then_inc(ids_loaded, 16)
            sp.dma_start(xT_sb[:, 0:HN], xT[:, 0:HN]).then_inc(x_loaded[0], 16)
            sp.dma_start(style_sb[:, :], style).then_inc(style_loaded, 16)
            sp.dma_start(ln0_sb[:, :, :], ln_row.rearrange("a b d -> a (b d)")[0, :].partition_broadcast(P)
                         ).then_inc(ln0_loaded, 16)
            for e in range(2):
                sp.dma_start(w_raw[:, e, :], w_all[:, e, :]).then_inc(w_loaded[e], 16)
            sp.dma_start(w_raw[:, 2:E, :], w_all[:, 2:E, :]).then_inc(w_loaded[2], 16)
            sp.wait_ge(gates_T_ready, 1)
            sp.dma_start(scratch.rearrange("e (j p) -> (e j) p", p=P), gates_T[:, :]).then_inc(gates_stored, 16)
            sp.wait_ge(gates_stored, 16)
            for first, end in ((0, 1), (1, 2), (3, 4), (2, 3), (4, E)):
                sp.dma_start(gate_all[:, first:end, :],
                             scratch[first:end, :].rearrange("e n -> (e n)").partition_broadcast(P)
                             ).then_inc(gate_loaded[first], 16)
            for b, samples in ((0, HB), (HB, 1), (HB + 1, 1)):
                sp.wait_ge(out_ready, b + samples)
                js = slice(b * T, (b + samples) * T)
                sp.dma_start(out_dram[:, js, :], out_sb[:, js, :]).then_inc(out_stored, 16)
            sp.wait_ge(out_stored, 16 * 3)

        @block.gpsimd
        def _(pool):
            steps = Count()

            def split_low(e, q):
                pool.wait_ge(w_high_ready, 4 * e + q + 1)
                nc.gpsimd.tensor_tensor(w_low[w_set(e)][:, quarter(q)], w_raw[:, e, quarter(q)],
                                        w_high[w_set(e)][:, quarter(q)].bitcast(F32), ALU.subtract
                                        ).then_inc(w_low_ready, 1)

            def add_block(e, h):
                pool.wait_ge(y_taken, HALVES * e + h + 1)
                nc.gpsimd.tensor_tensor(y_sum[:, h, :], y_sum[:, h, :], y_part[:, h, :], ALU.add).then_inc(y_added, 1)

            nc.gpsimd.memset(ident[:, :], 0.0).then_inc(pool_steps, steps.add())
            nc.gpsimd.iota(domain_no[:, :], pattern=[[1, DOMAINS]], base=0, channel_multiplier=0,
                           allow_small_or_imprecise_dtypes=True).then_inc(masks_ready, 1)
            pool.wait_ge(pool_steps, steps.n)
            nc.gpsimd.affine_select(out=ident[:, :], in_=ident[:, :], compare_op=ALU.not_equal, fill=1.0,
                                    base=0, pattern=[[-1, P]], channel_multiplier=1).then_inc(ident_ready, 1)
            nc.gpsimd.iota(lane[:, :], pattern=[[0, 1]], base=0, channel_multiplier=1,
                           allow_small_or_imprecise_dtypes=True).then_inc(masks_ready, 1)
            nc.gpsimd.memset(in_sample[:, :], 1.0).then_inc(pool_steps, steps.add())
            nc.gpsimd.memset(w_diag[:, :, :], 0.0).then_inc(masks_ready, 1)
            pool.wait_ge(pool_steps, steps.n)
            nc.gpsimd.affine_select(out=in_sample[:, :], in_=in_sample[:, :], compare_op=ALU.is_ge, fill=0.0,
                                    base=0, pattern=[[-A, B]], channel_multiplier=1).then_inc(pool_steps, steps.add())
            pool.wait_ge(pool_steps, steps.n)
            nc.gpsimd.affine_select(out=in_sample[:, :], in_=in_sample[:, :], compare_op=ALU.is_ge, fill=0.0,
                                    base=A - 1, pattern=[[A, B]], channel_multiplier=-1).then_inc(masks_ready, 1)
            nc.gpsimd.iota(rank[:, :], pattern=[[-1, E]], base=E, channel_multiplier=0,
                           allow_small_or_imprecise_dtypes=True).then_inc(masks_ready, 1)

            def split_hidden(q):
                slot = q % RING
                pool.wait_ge(hid_relu, relus_of(q))
                if not scalar_high(q):
                    pool.wait_ge(hid_round, rounds_of(q))
                nc.gpsimd.tensor_tensor(hid_low[:, slot, :], hid_full[:, slot, :], hid_high[:, slot, :].bitcast(F32),
                                        ALU.subtract).then_inc(hid_split_pool, 1)

            def gate_block(k):
                e, h = PRE_ORDER[k]
                pool.wait_ge(gate_loaded[e], 16)
                pool.wait_ge(y_taken, k + 1)
                gate = gate_all[:, e, h * HN:(h + 1) * HN]
                if e == 0:
                    nc.gpsimd.tensor_tensor(y_sum[:, h, :], y_raw[:, k, :], gate, ALU.mult).then_inc(first_added, 1)
                else:
                    pool.wait_ge(first_added, k)
                    nc.gpsimd.tensor_tensor(y_gated[:, :], y_raw[:, k, :], gate, ALU.mult).then_inc(y_gated_ready, 1)

            def add_gated(k):
                e, h = PRE_ORDER[k]
                pool.wait_ge(first_added, k)
                pool.wait_ge(y_gated_ready, sum(i > 0 for i, _ in PRE_ORDER[:k + 1]))
                nc.gpsimd.tensor_tensor(y_sum[:, h, :], y_sum[:, h, :], y_gated[:, :], ALU.add).then_inc(first_added, 1)

            def normalise(b):
                pool.wait_ge(z_affine, b + 1)
                for j in range(b * T, (b + 1) * T):
                    nc.gpsimd.tensor_scalar(z[:, j, :], x1[:, j, :], rstd[:, 1, j:j + 1], z_shift[:, j:j + 1],
                                            ALU.mult, ALU.add).then_inc(z_ready, 1)

            for q in range(4):
                split_low(0, q)
            normalise(0)
            for q in range(4):
                split_low(1, q)
            split_hidden(0)
            normalise(2)
            for q in POOL_SPLITS[1:]:
                if q == 22:
                    split_low(3, 0)
                split_hidden(q)
                if q == 12:
                    split_low(2, 0)
                if q == 14:
                    split_low(2, 1)
                    split_low(2, 2)
                if q == 16:
                    split_low(2, 3)
            split_low(3, 1)
            split_low(3, 2)
            gate_block(0)
            split_low(3, 3)
            gate_block(1)
            add_gated(1)
            split_low(4, 0)
            gate_block(2)
            gate_block(3)
            split_low(4, 1)
            add_gated(3)
            split_low(4, 2)
            add_block(3, 0)
            split_low(4, 3)
            pool.wait_ge(first_added, 4)
            add_block(3, 1)
            split_low(5, 0)
            split_low(5, 1)
            add_block(4, 0)
            for e in (5, 6):
                split_low(e, 2)
                split_low(e, 3)
                add_block(e - 1, 1)
                gate_block(e - 1)
                split_low(e + 1, 0)
                pool.wait_ge(y_added, HALVES * e - PRE_BLOCKS)
                add_gated(e - 1)
                split_low(e + 1, 1)
                pool.wait_ge(first_added, e)
                add_block(e, 0)
            split_low(E - 1, 2)
            split_low(E - 1, 3)
            add_block(E - 2, 1)
            add_block(E - 1, 0)

        @block.scalar
        def _(act):
            ac = nc.scalar.activation
            act.dma_start(tables_sb[:, :, :], tables).then_inc(tables_loaded, 16)
            act.dma_start(early_sb[:, :], early).then_inc(early_loaded, 16)
            act.dma_start(xT_sb[:, HN:N], xT[:, HN:N]).then_inc(x_loaded[1], 16)
            nc.scalar.preload_act_table(ACT.Gelu)
            act.wait_ge(early_loaded, 16)
            for b in range(B):
                rows = slice((b % HB) * SLOT, (b % HB) * SLOT + A)
                act.wait_ge(down_in_psum, b + 1)
                ac(hidden[rows, b // HB, :], down_ps[b // HB][rows, 0:S], ACT.Gelu,
                   bias=cols[rows, C_DB:C_DB + 1]).then_inc(gelu_ready, 1)
            nc.scalar.preload_act_table(ACT.Sqrt)
            roots = Count()

            def root(dst, src, scale, bias):
                roots.add()
                act.wait_ge(var_ready, roots.n)
                ac(dst, src, ACT.Sqrt, scale=scale, bias=bias).then_inc(std_ready, 1)

            def token_root(k, js):
                root(std[:, k, js], mv[:, k, js, 1], 1.0, eps[:, 0:1])

            def feature_root(h):
                bs = slice(h * HB, (h + 1) * HB)
                root(t_std[:, bs], t_mv[:, bs, 1], g2[:, 0:1], eps[:, 1:2])

            def tiles(b, n=1):
                return slice(b * T, (b + n) * T)

            def softplus():
                nc.scalar.preload_act_table_set("natural_log_exp_and_others")
                act.wait_ge(soft_in, 1)
                ac(soft[:, 1, :], soft[:, 0, :], ACT.Exp).then_inc(soft_exp, 1)
                act.wait_ge(soft_exp, 1)
                ac(soft[:, 2, :], soft[:, 1, :], ACT.Ln, bias=1.0).then_inc(soft_ln, 1)
                nc.scalar.preload_act_table(ACT.Sqrt)

            def round_h(b):
                act.wait_ge(affine_ready, b + 1)
                if b % HB == HB - 1:
                    act.wait_ge(h_full_ready, b)
                ac(h_high[:, b, :], zT_ps[b], ACT.Identity, bias=shift_T[:, b:b + 1],
                   scale=scale_T[:, b:b + 1]).then_inc(h_rounded, 1)

            def round_first_weights(e, quarters):
                act.wait_ge(w_loaded[e], 16)
                for q in quarters:
                    ac(w_high[e][:, quarter(q)], w_raw[:, e, quarter(q)], ACT.Copy).then_inc(w_high_ready, 1)

            def relu_unit(e, u, q=None, between=lambda: None):
                q = UNITS * e + u if q is None else q
                slot = u % RING
                act.wait_ge(hid_in_psum, q + 1)
                bias = cols[:, bass.ds(C_B1 + e * UNITS + u, 1)]
                ac(hid_full[:, slot, :], hid_ps[slot][:, :], ACT.Relu, bias=bias).then_inc(hid_relu, 1)
                between()
                if u % 2 == 0 or (isinstance(q, int) and q in EARLY_HIGHS):
                    ac(hid_high[:, slot, :], hid_ps[slot][:, :], ACT.Relu, bias=bias).then_inc(hid_relu, 1)

            def relu_pre(q, between=lambda: None):
                e, h = PRE_ORDER[q // FC]
                relu_unit(e, h * FC + q % FC, q, between)

            act.wait_ge(eps_ready, 1)
            token_root(0, tiles(0, 2))
            round_first_weights(0, range(4))
            act.wait_ge(style_in_psum, 4)
            ac(sty1_T[:, :], sty1_ps, ACT.Relu, bias=col(C_SB1, SC)).then_inc(style_ready, 1)
            act.wait_ge(style_in_psum, 6)
            ac(gamma_raw[:, :], gam_ps, ACT.Identity, bias=col(C_SBG)).then_inc(gamma_beta_ready, 1)
            ac(beta_T[:, :], bet_ps, ACT.Identity, bias=col(C_SBB)).then_inc(gamma_beta_ready, 1)
            token_root(1, tiles(0))
            token_root(1, tiles(1))
            softplus()
            feature_root(0)
            round_first_weights(1, range(2))
            round_h(0)
            round_h(1)
            token_root(0, tiles(2, 2))
            round_first_weights(1, range(2, 4))
            relu_pre(0)
            relu_pre(1, between=lambda: token_root(1, tiles(2)))
            relu_pre(2, between=lambda: token_root(1, tiles(3)))
            relu_pre(3)
            relu_pre(4)
            feature_root(1)
            relu_pre(5)
            round_h(2)
            round_h(3)
            for q in range(6, 11):
                relu_pre(q)
                if q == 8:
                    nc.scalar.preload_act_table(ACT.Exp)
            act.wait_ge(logits_shifted, 1)
            ac(gt[:, 1, :, :], gt[:, 0, :, :], ACT.Exp).then_inc(exps_ready, 1)
            for q in range(11, 22):
                relu_pre(q)
            act.wait_ge(gates_T_in_psum, 1)
            ac(gates_T[:, :], misc[1][0:E * J, 0:P], ACT.Copy).then_inc(gates_T_ready, 1)
            for q in range(22, PRE_UNITS):
                relu_pre(q)
            with act.Fori(3, E) as e:
                for u in range(UNITS):
                    relu_unit(e, u)

        @block.tensor
        def _(pe):
            mm = nc.tensor.matmul

            def down(b):
                if b % HB == 0:
                    pe.wait_ge(x_loaded[b // HB], 16)
                row = (b % HB) * SLOT
                mm(down_ps[b // HB][row:row + A, 0:S], EARLY.of(early_sb, "down"), xT_sb[:, b * S:(b + 1) * S],
                   start=True, stop=True, tile_position=(0, row)).then_inc(down_in_psum, 1)

            def residual(b):
                for t in range(T):
                    mm(sum_ps[b][:, t, :], xT_sb[:, (b * T + t) * P:(b * T + t + 1) * P], ident[:, :],
                       start=(t == 0), stop=False, skip_group_check=True)

            def up(b):
                pe.wait_ge(gelu_ready, b + 1)
                row = (b % HB) * SLOT
                for t in range(T):
                    last = mm(sum_ps[b][:, t, :], hidden[row:row + AUG, b // HB, t * P:(t + 1) * P],
                              up_eff[row:row + AUG, b // HB, :], start=False, stop=True, skip_group_check=True)
                last.then_inc(sum_in_psum, 1)

            def transpose_z(b):
                if b % HB == HB - 1:
                    pe.wait_ge(z_odd_ready, b // HB + 1)
                else:
                    pe.wait_ge(z_ready, T * (b // HB + 1))
                for t in range(T):
                    last = nc.tensor.transpose(zT_ps[b][:, t * P:(t + 1) * P], z[:, b * T + t, :], ident[:, :])
                last.then_inc(zT_in_psum, 1)

            def router(h):
                for j in range(h * HJ, (h + 1) * HJ):
                    last = mm(logit_ps[:, j, :], h_full[:, j // T, (j % T) * P:(j % T + 1) * P],
                              STYLE.of(style_sb, "router"), start=True, stop=True, skip_group_check=True)
                last.then_inc(logits_in_psum, 1)

            def high_pair(ps, k, w, moving_high, first):
                mm(ps, w_low[k][:, w], moving_high, start=first, stop=False)
                mm(ps, w_high[k][:, w], moving_high, start=False, stop=False)

            def half_of(t, u):
                return t[:, u // FC * HB:(u // FC + 1) * HB, :].rearrange("p b s -> p (b s)")

            def first_columns(u):
                return slice(u % FC * P, (u % FC + 1) * P)

            def first_highs(e, u):
                if u in (0, 2):
                    pe.wait_ge(w_low_ready, 4 * e + u // 2 + 1)
                high_pair(hid_ps[u % RING][:, :], w_set(e), first_columns(u), half_of(h_high, u), True)

            def first_low(e, u):
                mm(hid_ps[u % RING][:, :], w_high[w_set(e)][:, first_columns(u)], half_of(h_low, u),
                   start=False, stop=True).then_inc(hid_in_psum, 1)

            def first_product(e, u):
                first_highs(e, u)
                first_low(e, u)

            def second_product(e, u, q, blk, low_ready=None, between=lambda: None):
                half, c = u // FC, u % FC
                if half == 0 and c in (0, 2):
                    pe.wait_ge(w_low_ready, 4 * e + 2 + c // 2 + 1)
                if isinstance(q, int) and q < PRE_UNITS:
                    in_order = sum(is_pool(i) == is_pool(q) for i in range(q + 1))
                    low_ready = hid_split_pool if is_pool(q) else hid_split, in_order
                    if scalar_high(q):
                        pe.wait_ge(hid_relu, relus_of(q))
                    else:
                        pe.wait_ge(*low_ready)
                elif low_ready is None:
                    pe.wait_ge(hid_split, q + 1 - len(POOL_SPLITS))
                if c == 0 and not (isinstance(blk, int) and blk < 2):
                    pe.wait_ge(y_taken, blk - 1)
                ps, w, slot = y_ps[blk_parity(blk, u)][:, :], slice(FF + c * P, FF + (c + 1) * P), u % RING
                high_pair(ps, w_set(e), w, hid_high[:, slot, :], c == 0)
                between()
                if low_ready is not None:
                    pe.wait_ge(*low_ready)
                mm(ps, w_high[w_set(e)][:, w], hid_low[:, slot, :], start=False, stop=c == FC - 1
                   ).then_inc(down_done, 1)

            def blk_parity(blk, u):
                return blk % 2 if isinstance(blk, int) else u // FC

            def pre(part, q):
                e, h = PRE_ORDER[q // FC]
                part(e, h * FC + q % FC)

            def warm(n):
                for _ in range(n):
                    mm(bank[3][:, 0:P], ident[:, :], ident[:, :], start=True, stop=True)

            def pre_second(q, between=lambda: None):
                e, h = PRE_ORDER[q // FC]
                second_product(e, h * FC + q % FC, q, q // FC, between=between)

            pe.wait_ge(ident_ready, 1)
            warm(WARM_LOAD)
            pe.wait_ge(early_loaded, 16)
            down(0)
            down(1)
            pe.wait_ge(w_diag_ready, 1)
            for b in range(B):
                row = (b % HB) * SLOT
                last = mm(up_eff_ps[row:row + SLOT, (b // HB) * D:(b // HB + 1) * D], w_diag[:, b, :],
                          EARLY.of(early_sb, "up"), start=True, stop=True, tile_position=(0, row),
                          skip_group_check=True)
            last.then_inc(up_eff_in_psum, 1)
            pe.wait_ge(style_loaded, 16)
            pe.wait_ge(onehots_ready, 1)
            mm(se_ps, STYLE.of(style_sb, "subj", SUBJ), onehot_s[:, :], start=True, stop=True).then_inc(style_in_psum, 1)
            residual(0)
            down(2)
            down(3)
            pe.wait_ge(ones_ready, HB)
            pe.wait_ge(up_eff_ready, 1)
            up(0)
            residual(1)
            up(1)
            pe.wait_ge(style_ready, 1)
            mm(hyp1_ps, STYLE.of(style_sb, "hyp1", SE), se_T[:, :], start=True, stop=True).then_inc(style_in_psum, 1)
            pe.wait_ge(style_ready, 2)
            mm(hyp2_ps, STYLE.of(style_sb, "hyp2"), hyp1_T[:, :], start=True, stop=True).then_inc(style_in_psum, 1)
            residual(2)
            pe.wait_ge(style_ready, 3)
            mm(sty1_ps, STYLE.of(style_sb, "sty1"), hyp2_T[:, :], start=True, stop=True).then_inc(style_in_psum, 1)
            residual(3)
            pe.wait_ge(style_ready, 4)
            sty2 = STYLE.of(style_sb, "sty2", SC)
            mm(gam_ps, sty2[:, 0:D], sty1_T[:, :], start=True, stop=True).then_inc(style_in_psum, 1)
            mm(bet_ps, sty2[:, D:2 * D], sty1_T[:, :], start=True, stop=True).then_inc(style_in_psum, 1)
            up(2)
            up(3)
            warm(WARM_NORM[0])
            transpose_z(0)
            pe.wait_ge(soft_in, 1)
            transpose_z(1)
            warm(WARM_NORM[1])
            pe.wait_ge(h_rounded, HB)
            for q in range(2):
                pre(first_highs, q)
            pe.wait_ge(h_ready, 1)
            for q in range(2):
                pre(first_low, q)
            pre(first_product, 2)
            pre(first_product, 3)
            pe.wait_ge(sum_taken, T * HB + T)
            router(0)
            pre_second(0, between=lambda: pre(first_highs, 4))
            pre(first_low, 4)
            pre_second(1, between=lambda: transpose_z(2))
            pre(first_product, 5)
            transpose_z(3)
            pre_second(2)
            for q in range(6, 8):
                pre(first_product, q)
                pre_second(q - LEAD)

            def first_highs_8():
                pe.wait_ge(h_rounded, B)
                pre(first_highs, 8)
            pre_second(8 - LEAD, between=first_highs_8)
            pe.wait_ge(h_ready, HALVES)
            pre(first_low, 8)
            router(1)
            for q in range(9, 21):
                pre(first_product, q)
                pre_second(q - LEAD)
            pre(first_product, 21)
            pe.wait_ge(gates_ready, 1)
            nc.tensor.transpose(misc[1][0:E * J, 0:P], gates[:, :, :].rearrange("p e j -> p (e j)"), ident[:, :]
                                ).then_inc(gates_T_in_psum, 1)
            pre_second(21 - LEAD)
            for q in range(22, PRE_UNITS):
                pre(first_product, q)
                pre_second(q - LEAD)

            def expert(e):
                for u in range(UNITS):
                    first_product(e, u)
                    back = u < LEAD
                    second_product(e - back, (u - LEAD) % UNITS, UNITS * e + u - LEAD,
                                   HALVES * e - 1 if back else HALVES * e + (u - LEAD) // FC)

            for u in range(UNITS):
                first_product(3, u)
                if u < LEAD:
                    pre_second(PRE_UNITS - LEAD + u)
                else:
                    second_product(3, u - LEAD, PRE_UNITS + u - LEAD, PRE_BLOCKS + (u - LEAD) // FC)
            with pe.Fori(4, E) as e:
                expert(e)
            for u in range(UNITS - LEAD, UNITS - 1):
                second_product(E - 1, u, UNITS * (E - 1) + u, HALVES * E - 1)
            pe.wait_ge(hid_round, UNITS // 2 * E - len(EARLY_HIGHS))
            second_product(E - 1, UNITS - 1, UNITS * E - 1, HALVES * E - 1,
                           low_ready=(hid_split, UNITS * E - len(POOL_SPLITS)))
            pe.wait_ge(gates_T_ready, 1)
            pe.wait_ge(y_added, HALVES * (E - 1) + 1 - PRE_BLOCKS)
            for j in range(HJ):
                last = nc.tensor.transpose(misc[0][:, j * P:(j + 1) * P], y_sum[:, 0, j * P:(j + 1) * P], ident[:, :])
            last.then_inc(yT_in_psum, 1)
            pe.wait_ge(first_added, PRE_BLOCKS)
            for b in range(HB, B):
                for t in range(T):
                    j = (b - HB) * T + t
                    mm(sum_last[b - HB][:, t * P:(t + 1) * P], y_sum[:, 1, j * P:(j + 1) * P], ident[:, :],
                       start=(t == 0), stop=False, skip_group_check=True)
            for b in range(HB, B):
                pe.wait_ge(y_taken, HALVES * E - 1 + b - HB + 1)
                for t in range(T):
                    j = (b - HB) * T + t
                    last = mm(sum_last[b - HB][:, t * P:(t + 1) * P], y_part[:, 1, j * P:(j + 1) * P], ident[:, :],
                              start=False, stop=True, skip_group_check=True)
                last.then_inc(yT_in_psum, 1)

        @block.vector
        def _(ve):
            v = nc.vector
            steps = Count()

            def own():
                ve.wait_ge(vec_steps, steps.n)

            v.memset(eps[:, 0:1], LN_EPS)
            v.memset(eps[:, 1:2], IN_EPS).then_inc(eps_ready, 1)
            for b in range(HB):
                v.memset(hidden[b * SLOT + A:b * SLOT + A + 1, :, :], 1.0).then_inc(ones_ready, 1)
            ve.wait_ge(ident_ready, 1)
            v.tensor_reduce(eye_a[:, :], ident[:, :].rearrange("p (b a) -> p a b", b=B), AX, ALU.add
                            ).then_inc(vec_steps, steps.add())
            ve.wait_ge(ids_loaded, 16)
            v.tensor_copy(ids_f[:, :], ids_i[:, :]).then_inc(vec_steps, steps.add())
            own()
            v.tensor_scalar(dom[:, 0:1], ids_f[:, 0:1], 0.0, None, ALU.is_ge).then_inc(vec_steps, steps.add())
            v.tensor_scalar(dom[:, 1:2], ids_f[:, 0:1], 0.0, float(DOMAINS - 1), ALU.max, ALU.min
                            ).then_inc(vec_steps, steps.add())
            v.tensor_scalar(subj[:, 0, :], ids_f[0:SUBJ, 1:1 + B], 0.0, float(SUBJ), ALU.is_lt, ALU.mult
                            ).then_inc(vec_steps, steps.add())
            own()
            v.scalar_tensor_tensor(dom[:, 2:3], ids_f[:, 0:1], float(DOMAINS), dom[:, 0:1], ALU.is_lt, ALU.mult
                                   ).then_inc(vec_steps, steps.add())
            ve.wait_ge(masks_ready, 2)
            v.tensor_scalar(pick[:, 0, :], domain_no[:, :], dom[:, 1:2], None, ALU.is_equal
                            ).then_inc(vec_steps, steps.add())
            v.tensor_tensor(subj[:, 1, :], subj[:, 0, :], ids_f[0:SUBJ, 1:1 + B], ALU.add).then_inc(vec_steps, steps.add())
            own()
            v.tensor_scalar(pick[:, 1, :], pick[:, 0, :], dom[:, 2:3], None, ALU.mult).then_inc(vec_steps, steps.add())
            v.tensor_scalar(dom[:, 3:4], dom[:, 2:3], -1.0, 1.0, ALU.mult, ALU.add).then_inc(vec_steps, steps.add())
            v.tensor_scalar(subj[:, 2, :], subj[:, 1, :], 0.0, float(SUBJ - 1), ALU.max, ALU.min
                            ).then_inc(vec_steps, steps.add())
            ve.wait_ge(tables_loaded, 16)
            own()
            v.tensor_tensor(picked[:, 0:AUG, :], tables_sb[:, 0:AUG, :],
                            pick[:, 1, :].unsqueeze(1).broadcast_to([P, AUG, DOMAINS]), ALU.mult
                            ).then_inc(vec_steps, steps.add())
            v.tensor_tensor(picked[:, AUG, :], tables_sb[:, AUG, :], pick[:, 0, :], ALU.mult
                            ).then_inc(vec_steps, steps.add())
            v.tensor_scalar(onehot_s[:, :], subj[:, 2, :], lane[0:SUBJ, :], None, ALU.is_equal).then_inc(onehots_ready, 1)
            own()
            v.tensor_reduce(w_sel[:, :], picked[:, :, :], AX, ALU.add).then_inc(vec_steps, steps.add())
            own()
            v.scalar_tensor_tensor(w_eff[:, 0:A], eye_a[:, :], dom[:, 3:4], w_sel[:, 0:A], ALU.mult, ALU.add
                                   ).then_inc(vec_steps, steps.add())
            v.tensor_tensor(w_eff[:, A:AUG], w_sel[:, A:AUG], w_sel[:, AUG:GROUPS], ALU.add
                            ).then_inc(vec_steps, steps.add())
            ve.wait_ge(masks_ready, 4)
            own()
            v.tensor_tensor(w_diag[:, :, 0:AUG], w_eff[:, :].unsqueeze(1).broadcast_to([P, B, AUG]),
                            in_sample[:, :].unsqueeze(2).broadcast_to([P, B, AUG]), ALU.mult).then_inc(w_diag_ready, 1)
            ve.wait_ge(early_loaded, 16)
            v.tensor_scalar(g2[:, :], col(C_LNG), col(C_LNG), None, ALU.mult).then_inc(vec_steps, steps.add())
            ve.wait_ge(up_eff_in_psum, 1)
            v.tensor_tensor(up_eff[:, :, :], up_eff_ps.rearrange("p (h d) -> p h d", d=D),
                            EARLY.of(early_sb, "up_b").unsqueeze(1).broadcast_to([P, HALVES, D]), ALU.add
                            ).then_inc(up_eff_ready, 1)

            def style_step(k):
                ve.wait_ge(style_in_psum, k + 1)
                if k == 0:
                    v.tensor_copy(se_T[:, :], se_ps).then_inc(style_ready, 1)
                elif k == 1:
                    v.tensor_scalar(hyp1_T[:, :], hyp1_ps, col(C_HB1), 0.0, ALU.add, ALU.max).then_inc(style_ready, 1)
                else:
                    v.tensor_scalar(hyp2_T[:, :], hyp2_ps, col(C_HB2), None, ALU.add).then_inc(style_ready, 1)

            def minus_abs():
                ve.wait_ge(gamma_beta_ready, 2)
                v.scalar_tensor_tensor(soft[:, 0, :], gamma_raw[:, :], -1.0, gamma_raw[:, :], ALU.mult, ALU.min
                                       ).then_inc(soft_in, 1)

            def softplus(k):
                if k == 0:
                    ve.wait_ge(soft_ln, 1)
                    v.scalar_tensor_tensor(gamma_T[:, :], gamma_raw[:, :], 0.0, soft[:, 2, :], ALU.max, ALU.add
                                           ).then_inc(vec_steps, steps.add())
                elif k == 1:
                    after("softplus")
                    v.tensor_scalar(gamma_T[:, :], gamma_T[:, :], 1e-8, None, ALU.add).then_inc(vec_steps, steps.add())
                else:
                    after("softplus")
                    v.tensor_scalar(gamma_g[:, :], gamma_T[:, :], col(C_LNG), None, ALU.mult
                                    ).then_inc(vec_steps, steps.add())
                mark["softplus"] = steps.n

            mark = {}
            asked = Count()
            root_of = {}

            def after(stage):
                ve.wait_ge(vec_steps, mark[stage])

            def ask(key):
                asked.add()
                root_of[key] = asked.n

            def tiles(b, n=1):
                return range(b * T, (b + n) * T)

            def token_stats(k, b, src):
                for j in tiles(b):
                    v.bn_stats(stats[:, k, j, :], src(j)).then_inc(vec_steps, steps.add())
                mark["stats", k, b] = steps.n

            def token_mv(k, b, n=1):
                for i in range(n * T):
                    token_mv_step(k, b, n, i)

            def token_mv_step(k, b, n, i):
                j = b * T + i
                after(("stats", k, j // T))
                last = v.bn_aggr(mv[:, k, j, :], stats[:, k, j, :])
                if i < n * T - 1:
                    last.then_inc(vec_steps, steps.add())
                else:
                    ask(("token", k, b))
                    last.then_inc(var_ready, 1)

            def sum_stats(b):
                ve.wait_ge(sum_in_psum, b + 1)
                token_stats(0, b, lambda j: sum_ps[b][:, j % T, :])

            def sum_rstd(h):
                js = slice(h * HJ, (h + 1) * HJ)
                ve.wait_ge(std_ready, root_of["token", 0, h * HB])
                v.reciprocal(rstd[:, 0, js], std[:, 0, js]).then_inc(vec_steps, steps.add())
                mark["sum_rstd", h] = steps.n

            def centre(b):
                ve.wait_ge(var_ready, root_of["token", 0, b // HB * HB])
                for j in tiles(b):
                    v.scalar_tensor_tensor(centred[:, j, :], sum_ps[b][:, j % T, :], mv[:, 0, j, 0:1],
                                           ln0_sb[:, 0, :], ALU.subtract, ALU.mult).then_inc(sum_taken, 1)

            def adapter_out(b):
                after(("sum_rstd", b // HB))
                for j in tiles(b):
                    ve.wait_ge(sum_taken, j + 1)
                    v.scalar_tensor_tensor(x1[:, j, :], centred[:, j, :], rstd[:, 0, j:j + 1], ln0_sb[:, 1, :],
                                           ALU.mult, ALU.add).then_inc(vec_steps, steps.add())
                mark["x1", b] = steps.n

            def x1_stats(b, between=None):
                after(("x1", b))
                for j in tiles(b):
                    v.bn_stats(stats[:, 1, j, :], x1[:, j, :]).then_inc(vec_steps, steps.add())
                    if between is not None and j == b * T:
                        between()
                mark["stats", 1, b] = steps.n

            def x1_rstd(b):
                js = slice(b * T, (b + 1) * T)
                ve.wait_ge(std_ready, root_of["token", 1, b])
                v.reciprocal(rstd[:, 1, js], std[:, 1, js]).then_inc(vec_steps, steps.add())
                mark["x1_rstd", b] = steps.n

            def x1_shift(b):
                js = slice(b * T, (b + 1) * T)
                after(("x1_rstd", b))
                v.scalar_tensor_tensor(z_shift[:, js], mv[:, 1, js, 0], -1.0, rstd[:, 1, js], ALU.mult, ALU.mult
                                       ).then_inc(z_affine, 1)

            def feature_stats(b):
                ve.wait_ge(zT_in_psum, b + 1)
                v.bn_stats(t_stats[:, b, :], zT_ps[b]).then_inc(vec_steps, steps.add())
                mark["f_stats", b] = steps.n

            def feature_mv(h):
                for b in range(h * HB, (h + 1) * HB):
                    after(("f_stats", b))
                    last = v.bn_aggr(t_mv[:, b, :], t_stats[:, b, :])
                    if b % HB < HB - 1:
                        last.then_inc(vec_steps, steps.add())
                last.then_inc(var_ready, 1)
                ask(("feature", h))

            def normalise(b):
                ve.wait_ge(z_affine, b + 1)
                for j in tiles(b):
                    last = v.tensor_scalar(z[:, j, :], x1[:, j, :], rstd[:, 1, j:j + 1], z_shift[:, j:j + 1],
                                           ALU.mult, ALU.add)
                    if j % T < T - 1:
                        last.then_inc(vec_steps, steps.add())
                last.then_inc(z_odd_ready, 1)

            def feature_affine(h, between=lambda k: None):
                bs = slice(h * HB, (h + 1) * HB)
                ve.wait_ge(var_ready, root_of["feature", h])
                v.tensor_scalar(t_off[:, bs], t_mv[:, bs, 0], col(C_LNG), col(C_LNB), ALU.mult, ALU.add
                                ).then_inc(vec_steps, steps.add())
                mark["f_mean", h] = steps.n
                between(0)
                after(("f_mean", h))
                v.tensor_scalar(t_off[:, bs], t_off[:, bs], -1.0, col(C_LNB), ALU.mult, ALU.add
                                ).then_inc(vec_steps, steps.add())
                ve.wait_ge(std_ready, root_of["feature", h])
                v.reciprocal(t_rstd[:, bs], t_std[:, bs]).then_inc(vec_steps, steps.add())
                mark["f_rstd", h] = steps.n
                between(1)
                after(("f_rstd", h))
                v.tensor_tensor(t_gain[:, bs], gamma_T[:, bs], t_rstd[:, bs], ALU.mult).then_inc(vec_steps, steps.add())
                mark["f_gain", h] = steps.n
                v.tensor_tensor(scale_T[:, bs], gamma_g[:, bs], t_rstd[:, bs], ALU.mult).then_inc(vec_steps, steps.add())
                between(2)
                after(("f_gain", h))
                for b in range(h * HB, (h + 1) * HB):
                    v.scalar_tensor_tensor(shift_T[:, b:b + 1], t_off[:, b:b + 1], t_gain[:, b:b + 1],
                                           beta_T[:, b:b + 1], ALU.mult, ALU.add).then_inc(affine_ready, 1)

            def full_h(b):
                if b % HB == HB - 1:
                    ve.wait_ge(affine_ready, (b // HB + 1) * HB)
                else:
                    ve.wait_ge(h_rounded, b + 1)
                v.tensor_scalar(h_full[:, b, :], zT_ps[b], scale_T[:, b:b + 1], shift_T[:, b:b + 1], ALU.mult, ALU.add
                                ).then_inc(h_full_ready, 1)

            def low_h(b):
                ve.wait_ge(h_full_ready, (b // HB + 1) * HB)
                ve.wait_ge(h_rounded, b + 1)
                last = v.tensor_tensor(h_low[:, b, :], h_full[:, b, :], h_high[:, b, :].bitcast(F32), ALU.subtract)
                if b % HB == HB - 1:
                    last.then_inc(h_ready, 1)
                else:
                    last.then_inc(vec_steps, steps.add())

            def round_weights(e, q, products, value):
                ve.wait_ge(w_loaded[2], 16)
                ve.wait_ge(products, value)
                v.tensor_copy(w_high[0][:, quarter(q)],
                              w_raw[:, bass.ds(e, 1), quarter(q)].rearrange("p a n -> p (a n)")).then_inc(w_high_ready, 1)

            def split_hidden(u, relus, rounds, own_high):
                slot = u % RING
                ve.wait_ge(hid_relu, relus)
                if own_high:
                    v.tensor_copy(hid_high[:, slot, :], hid_full[:, slot, :]).then_inc(hid_round, 1)
                    ve.wait_ge(hid_round, rounds)
                v.tensor_tensor(hid_low[:, slot, :], hid_full[:, slot, :], hid_high[:, slot, :].bitcast(F32),
                                ALU.subtract).then_inc(hid_split, 1)

            def split_pre(q):
                if is_pool(q):
                    if not scalar_high(q):
                        ve.wait_ge(hid_relu, relus_of(q))
                        v.tensor_copy(hid_high[:, q % RING, :], hid_full[:, q % RING, :]).then_inc(hid_round, 1)
                else:
                    split_hidden(q, relus_of(q), rounds_of(q), not scalar_high(q))

            def split_loop(e, u):
                split_hidden(u, UNITS // 2 * 3 * e + u // 2 * 3 + 2 + u % 2 + len(EARLY_HIGHS),
                             UNITS // 2 * e + u // 2 + 1 - len(EARLY_HIGHS), u % 2 == 1)

            def take_pre(k):
                ve.wait_ge(down_done, FC * (k + 1))
                v.tensor_scalar(y_raw[:, k, :], y_ps[k % 2][:, :], col(C_B2 + PRE_ORDER[k][0]), None, ALU.add
                                ).then_inc(y_taken, 1)

            def take_block(e, h):
                ve.wait_ge(down_done, UNITS * e + FC * (h + 1))
                if not (isinstance(e, int) and e == 3):
                    ve.wait_ge(y_added, HALVES * e + h - 1 - PRE_BLOCKS)
                v.scalar_tensor_tensor(y_part[:, h, :], y_ps[h][:, :], cols[:, bass.ds(C_B2 + e, 1)],
                                       gate_all[:, bass.ds(e, 1), h * HN:(h + 1) * HN].rearrange("p a n -> p (a n)"),
                                       ALU.add, ALU.mult).then_inc(y_taken, 1)

            style_step(0)
            sum_stats(0)
            sum_stats(1)
            style_step(1)
            token_mv(0, 0, HB)
            style_step(2)
            ve.wait_ge(ln0_loaded, 16)
            centre(0)
            sum_rstd(0)
            adapter_out(0)
            centre(1)
            x1_stats(0)
            adapter_out(1)
            token_mv(1, 0)
            x1_stats(1)
            minus_abs()
            token_mv(1, 1)
            x1_rstd(0)
            x1_shift(0)
            x1_rstd(1)
            sum_stats(2)
            x1_shift(1)
            normalise(1)
            sum_stats(3)
            softplus(0)
            feature_stats(0)
            feature_stats(1)
            softplus(1)
            feature_mv(0)
            softplus(2)
            feature_affine(0, between=lambda k: token_mv_step(0, HB, HB, k))
            token_mv_step(0, HB, HB, 3)
            full_h(1)
            full_h(0)
            low_h(0)
            low_h(1)
            sum_rstd(1)
            centre(2)
            adapter_out(2)
            x1_stats(2)
            centre(3)
            token_mv(1, 2)
            adapter_out(3)
            x1_rstd(2)
            x1_stats(3, between=lambda: x1_shift(2))
            token_mv(1, 3)
            split_pre(1)
            x1_rstd(3)
            x1_shift(3)
            normalise(3)
            feature_stats(2)
            feature_stats(3)
            feature_mv(1)
            feature_affine(1)
            full_h(3)
            full_h(2)
            low_h(2)
            low_h(3)
            split_pre(5)
            split_pre(7)
            take_pre(0)

            def bc(a):
                return a.unsqueeze(2).broadcast_to([P, J, E])

            rank_b = rank[:, :].unsqueeze(1).broadcast_to([P, J, E])

            def g_shift():
                ve.wait_ge(logits_in_psum, HALVES)
                v.tensor_reduce(gs[:, 0, :], logit_ps, AX, ALU.max).then_inc(vec_steps, steps.add())
                own()
                v.tensor_tensor(gt[:, 0, :, :], logit_ps, bc(gs[:, 0, :]), ALU.subtract).then_inc(logits_shifted, 1)

            def g_probs():
                ve.wait_ge(exps_ready, 1)
                v.tensor_reduce(gs[:, 1, :], gt[:, 1, :, :], AX, ALU.add).then_inc(vec_steps, steps.add())
                own()
                v.reciprocal(gs[:, 2, :], gs[:, 1, :]).then_inc(vec_steps, steps.add())
                own()
                v.tensor_tensor(gt[:, 2, :, :], gt[:, 1, :, :], bc(gs[:, 2, :]), ALU.mult).then_inc(vec_steps, steps.add())
                own()

            def g_top(src, best, hit, at, onehot):
                v.tensor_reduce(best, src, AX, ALU.max).then_inc(vec_steps, steps.add())
                own()
                v.tensor_tensor(hit, src, bc(best), ALU.is_equal).then_inc(vec_steps, steps.add())
                own()
                v.tensor_tensor(hit, hit, rank_b, ALU.mult).then_inc(vec_steps, steps.add())
                own()
                v.tensor_reduce(at, hit, AX, ALU.max).then_inc(vec_steps, steps.add())
                own()
                v.tensor_tensor(onehot, rank_b, bc(at), ALU.is_equal).then_inc(vec_steps, steps.add())
                own()

            def g_first():
                g_top(gt[:, 2, :, :], gs[:, 3, :], gt[:, 3, :, :], gs[:, 4, :], gt[:, 4, :, :])
                v.scalar_tensor_tensor(gt[:, 5, :, :], gt[:, 4, :, :], -2.0, gt[:, 2, :, :], ALU.mult, ALU.add
                                       ).then_inc(vec_steps, steps.add())
                own()

            def g_second():
                g_top(gt[:, 5, :, :], gs[:, 5, :], gt[:, 6, :, :], gs[:, 6, :], gt[:, 7, :, :])

            def g_renorm():
                v.tensor_tensor(gs[:, 7, :], gs[:, 3, :], gs[:, 5, :], ALU.add).then_inc(vec_steps, steps.add())
                own()
                v.reciprocal(gs[:, 7, :], gs[:, 7, :]).then_inc(vec_steps, steps.add())
                own()
                v.tensor_tensor(gs[:, 8, :], gs[:, 3, :], gs[:, 7, :], ALU.mult).then_inc(vec_steps, steps.add())
                v.tensor_tensor(gs[:, 9, :], gs[:, 5, :], gs[:, 7, :], ALU.mult).then_inc(vec_steps, steps.add())
                own()
                v.tensor_tensor(gt[:, 4, :, :], gt[:, 4, :, :], bc(gs[:, 8, :]), ALU.mult).then_inc(vec_steps, steps.add())
                v.tensor_tensor(gt[:, 7, :, :], gt[:, 7, :, :], bc(gs[:, 9, :]), ALU.mult).then_inc(vec_steps, steps.add())
                own()
                v.tensor_tensor(gates[:, :, :].rearrange("p e j -> p j e"), gt[:, 4, :, :], gt[:, 7, :, :], ALU.add).then_inc(gates_ready, 1)

            g_shift()
            split_pre(9)
            split_pre(10)
            split_pre(11)
            take_pre(1)
            g_probs()
            round_weights(2, 0, hid_in_psum, 10)
            split_pre(12)
            round_weights(2, 1, hid_in_psum, 12)
            split_pre(13)
            g_first()
            round_weights(2, 2, down_done, 10)
            split_pre(14)
            split_pre(15)
            take_pre(2)
            round_weights(2, 3, down_done, 12)
            split_pre(16)
            split_pre(17)
            g_second()
            g_renorm()
            split_pre(18)
            split_pre(19)
            take_pre(3)
            split_pre(20)
            round_weights(3, 0, hid_in_psum, UNITS * 2 + 6)
            split_pre(21)
            split_pre(22)
            take_pre(4)
            round_weights(3, 1, hid_in_psum, UNITS * 2 + 8)
            split_pre(23)

            def expert(e, last=False):
                round_weights(e, 2, down_done, UNITS * e - 2)
                split_loop(e, 0)
                split_loop(e, 1)
                round_weights(e, 3, down_done, UNITS * e)
                split_loop(e, 2)
                if isinstance(e, int) and e == 3:
                    take_pre(PRE_BLOCKS - 1)
                else:
                    take_block(e - 1, 1)
                split_loop(e, 3)
                split_loop(e, 4)
                if not last:
                    round_weights(e + 1, 0, hid_in_psum, UNITS * e + 6)
                split_loop(e, 5)
                if last:
                    take_block(e, 0)
                split_loop(e, 6)
                if isinstance(e, int) and e in (3, 4):
                    ve.wait_ge(gate_loaded[e], 16)
                if not last:
                    take_block(e, 0)
                    round_weights(e + 1, 1, hid_in_psum, UNITS * e + 8)
                split_loop(e, 7)

            expert(3)
            expert(4)
            with ve.Fori(5, E - 1) as e:
                expert(e)
            expert(E - 1, last=True)
            ve.wait_ge(down_done, UNITS * E)
            ve.wait_ge(y_added, HALVES * (E - 1) - PRE_BLOCKS)
            for b in range(HB, B):
                s = slice((b - HB) * S, (b - HB + 1) * S)
                v.scalar_tensor_tensor(y_part[:, 1, s], y_ps[1][:, s], col(C_B2 + E - 1),
                                       gate_all[:, E - 1, b * S:(b + 1) * S], ALU.add, ALU.mult).then_inc(y_taken, 1)
            for b, ps in enumerate((misc[0][:, 0:S], misc[0][:, S:2 * S], sum_last[0][:, 0:S], sum_last[1][:, 0:S])):
                ve.wait_ge(yT_in_psum, max(b, 1))
                v.tensor_tensor(out_sb[:, b * T:(b + 1) * T, :], ps.rearrange("p (t d) -> p t d", d=D),
                                x1[:, b * T:(b + 1) * T, :], ALU.add).then_inc(out_ready, 1)


def _padded(a):
    a = np.asarray(a)
    full = np.zeros((P,) + a.shape[1:], a.dtype)
    full[:a.shape[0]] = a
    return full


def _column(a):
    return _padded(np.reshape(a, (-1, 1)))


def _slots(a):
    full = np.zeros((HB, SLOT), np.asarray(a).dtype)
    full[:, :A] = np.asarray(a)
    return full.reshape(P, 1)


def kernel(x, itok_B_0_15, itok_B_6_14, L0_cond_down_W, L0_cond_down_b, L0_cond_up_W, L0_cond_up_b,
           L0_cond_expert_W, L0_cond_expert_b, L0_cond_domain_emb, L0_cond_ln_gamma, L0_cond_ln_beta,
           L1_cond_ln_g, L1_cond_ln_b, L1_cond_subj_emb, L1_cond_hyp_w1, L1_cond_hyp_b1, L1_cond_hyp_w2,
           L1_cond_hyp_b2, L1_cond_sty_w1, L1_cond_sty_b1, L1_cond_sty_w2, L1_cond_sty_b2, L1_cond_router_w,
           L1_cond_exp_w1, L1_cond_exp_b1, L1_cond_exp_w2, L1_cond_exp_b2):
    import concourse.bacc as bacc
    from concourse.bass_utils import run_bass_kernel_spmd

    f = {k: np.asarray(v) for k, v in dict(
        down=L0_cond_down_W, up=L0_cond_up_W, expert=L0_cond_expert_W, b1=L1_cond_exp_b1, w1=L1_cond_exp_w1,
        w2=L1_cond_exp_w2).items()}
    b1 = np.repeat(f["b1"].reshape(E, 1, FC, P), HALVES, axis=1).reshape(E * UNITS, P).T
    cols = np.concatenate([b1, np.asarray(L1_cond_exp_b2).T, _column(L1_cond_ln_g),
                           _column(L1_cond_ln_b), _column(L1_cond_hyp_b1), _column(L1_cond_hyp_b2),
                           _column(L1_cond_sty_b1), _column(L1_cond_sty_b2[:D]), _column(L1_cond_sty_b2[D:]),
                           _slots(L0_cond_down_b)], axis=1)
    up_b = np.zeros((P, D), f["up"].dtype)
    up_b[A::SLOT] = np.asarray(L0_cond_up_b)
    early = np.concatenate([f["down"].T, cols, np.tile(f["up"].T, (B, 1)), up_b], axis=1)
    tables = np.concatenate([f["expert"].transpose(1, 2, 0), np.asarray(L0_cond_expert_b).T[:, None, :],
                             np.asarray(L0_cond_domain_emb).T[:, None, :]], axis=1)
    tables = np.tile(tables, (B, 1, 1))
    ids = np.concatenate([np.repeat(np.asarray(itok_B_0_15), A).reshape(P, 1),
                          np.tile(np.asarray(itok_B_6_14), (P, 1))], axis=1)
    style = np.concatenate([_padded(L1_cond_subj_emb), _padded(L1_cond_hyp_w1), np.asarray(L1_cond_hyp_w2),
                            np.asarray(L1_cond_sty_w1), _padded(L1_cond_sty_w2), np.asarray(L1_cond_router_w)], axis=1)
    w_all = np.concatenate([f["w1"].transpose(1, 0, 2),
                            f["w2"].reshape(E, FC, P, D).transpose(2, 0, 1, 3).reshape(P, E, FF)], axis=2)
    arrays = {
        "xT": np.asarray(x).reshape(N, D).T,
        "ids": ids, "tables": tables, "early": early, "style": style,
        "ln_row": np.stack([np.asarray(L0_cond_ln_gamma), np.asarray(L0_cond_ln_beta)]).reshape(1, 2, D),
        "w_all": w_all,
    }
    arrays = {k + "_dram": np.ascontiguousarray(v) for k, v in arrays.items()}
    nc = bacc.Bacc("TRN2", target_bir_lowering=False, num_devices=1)
    args = [nc.dram_tensor(k, v.shape, mybir.dt.from_np(v.dtype), kind="ExternalInput").ap()
            for k, v in arrays.items()]
    args.append(nc.dram_tensor("out_dram", (B, S, D), F32, kind="ExternalOutput").ap())
    adapter_moe(nc, *args)
    result = run_bass_kernel_spmd(nc, [arrays], core_ids=[0])
    return result.results[0]["out_dram"]
```
